# Optimizing a Trainium2 kernel written in Bass

```python
import numpy as np
import jax
import jax.numpy as jnp

def _softmax(x, axis=-1):
    return jax.nn.softmax(x, axis=axis)

def _gelu(x):
    return jax.nn.gelu(x, approximate=True)

def _silu(x):
    return jax.nn.silu(x)

def _sigmoid(x):
    return jax.nn.sigmoid(x)

def _layernorm(x, axis=-1, eps=1e-05):
    m = jnp.mean(x, axis=axis, keepdims=True)
    v = jnp.var(x, axis=axis, keepdims=True)
    return (x - m) / jnp.sqrt(v + eps)

def _scatter_add(tgt, idx, src, axis=0):
    return tgt.at[idx].add(src)

def _segment_sum(src, seg, n):
    return jax.ops.segment_sum(src, seg, n)
kernel_name = 'mk_gnn_resnorm_d1_gnn_r8_a9337d'

def setup_inputs(seed: int=0):
    np.random.seed(seed)
    _w = jnp.asarray

    def _rec_inputs():
        import jax
        import jax.numpy as jnp
        _gk = jax.random.key(seed)
        x = -0.000202 + 1 * jax.random.normal(jax.random.fold_in(_gk, 1), (12500, 64), jnp.float32)
        _s = jax.random.randint(jax.random.fold_in(_gk, 2), (100000,), 0, 12500, jnp.int32)
        _d = jax.random.randint(jax.random.fold_in(_gk, 3), (100000,), 0, 12500, jnp.int32)
        _loop = jnp.arange(12500, dtype=jnp.int32)
        src = jnp.concatenate([_s, _d, _loop])
        dst = jnp.concatenate([_d, _s, _loop])
        _o = jnp.argsort(dst, stable=True)
        src = src[_o]
        dst = dst[_o]
        edge_attr_16 = -5.3897e-05 + 0.999841 * jax.random.normal(jax.random.fold_in(_gk, 11), (212500, 16), jnp.float32)
        return (x, src, dst, edge_attr_16)
    x, src, dst, edge_attr_16 = _rec_inputs()

    def _L0_gnn_setup():
        import jax, jax.numpy as jnp
        import numpy as np
        N, E, D, ED, H, O = (12500, 200000, 64, 16, 64, 64)
        key = jax.random.key(seed)
        ks = jax.random.split(key, 8)
        fan_in = 2 * D + ED
        s = 1.0 / np.sqrt(fan_in)
        return {'x': jax.random.normal(ks[0], (N, D), dtype=jnp.float32), 'edge_attr': jax.random.normal(ks[1], (E, ED), dtype=jnp.float32), 'edge_index': jax.random.randint(ks[2], (2, E), 0, N, dtype=jnp.int32), 'W1': jax.random.normal(ks[3], (fan_in, H), dtype=jnp.float32) * s, 'b1': jnp.zeros((H,), dtype=jnp.float32), 'W2': jax.random.normal(ks[4], (2 * H + ED, H), dtype=jnp.float32) * s, 'b2': jnp.zeros((H,), dtype=jnp.float32), 'W3': jax.random.normal(ks[5], (2 * H + ED, O), dtype=jnp.float32) * s, 'b3': jnp.zeros((O,), dtype=jnp.float32)}
    _L0_gnn_all = _L0_gnn_setup()
    _L0_gnn_in = {k: v for k, v in _L0_gnn_all.items() if k in ('W1', 'b1', 'W2', 'b2', 'W3', 'b3')}
    del _L0_gnn_all
    return {'x': x, 'src': src, 'dst': dst, 'edge_attr_16': edge_attr_16, 'L0_gnn_W1': _L0_gnn_in['W1'], 'L0_gnn_b1': _L0_gnn_in['b1'], 'L0_gnn_W2': _L0_gnn_in['W2'], 'L0_gnn_b2': _L0_gnn_in['b2'], 'L0_gnn_W3': _L0_gnn_in['W3'], 'L0_gnn_b3': _L0_gnn_in['b3']}

def reference(x, src, dst, edge_attr_16, L0_gnn_W1, L0_gnn_b1, L0_gnn_W2, L0_gnn_b2, L0_gnn_W3, L0_gnn_b3):
    import jax
    import jax.numpy as jnp

    def _L0_gnn_ref(x, edge_attr, edge_index, W1, b1, W2, b2, W3, b3):
        import jax, jax.numpy as jnp
        import numpy as np
        N, E, D, ED, H, O = (12500, 200000, 64, 16, 64, 64)
        src = edge_index[0]
        dst = edge_index[1]
        n_nodes = x.shape[0]

        def conv(h, W, b):
            m = jnp.concatenate([h[dst], h[src], edge_attr], axis=1) @ W + b
            return jax.ops.segment_sum(m, dst, num_segments=n_nodes)
        h = jax.nn.relu(conv(x, W1, b1))
        h = jax.nn.relu(conv(h, W2, b2))
        return conv(h, W3, b3)
    edge_index = jnp.stack([src, dst])
    x = _layernorm(x + _L0_gnn_ref(x, edge_attr_16, edge_index, L0_gnn_W1, L0_gnn_b1, L0_gnn_W2, L0_gnn_b2, L0_gnn_W3, L0_gnn_b3), axis=-1)
    return x

_drawn_inputs = setup_inputs


def setup_inputs(seed=0):
    import zlib

    import numpy as np

    out = dict(_drawn_inputs(seed))
    spreads = {'L0_gnn_b1': (0.0, 0.1), 'L0_gnn_b2': (0.0, 0.577), 'L0_gnn_b3': (0.0, 0.8)}
    factors = {}
    for name, (base, spread) in spreads.items():
        noise = np.random.default_rng([zlib.crc32(name.encode()), seed]).standard_normal(out[name].shape)
        drawn = base * np.exp(spread * noise) if base else spread * noise
        out[name] = jnp.asarray(drawn.astype(out[name].dtype))
    for name, factor in factors.items():
        out[name] = (out[name] * factor).astype(out[name].dtype)
    return out
```

```python
import concourse.bass as bass
from concourse import mybir
from contextlib import ExitStack


def gnn_kernel(nc, x, src, dst, edge_attr, weights, out):
    fp32 = mybir.dt.float32
    i32 = mybir.dt.int32
    ALU = mybir.AluOpType
    ACT = mybir.ActivationFunctionType
    X = mybir.AxisListType.X

    N, D = x.shape
    E, ED = edge_attr.shape
    P = nc.NUM_PARTITIONS
    LAYERS = len(weights)
    TILES = -(-N // P)
    NP = TILES * P
    NODE_REST = N - (TILES - 1) * P
    J = 16
    GROUP = P * J
    GROUPS = -(-E // GROUP)
    RING = 4
    ROUNDS = GROUPS // RING
    assert GROUPS == ROUNDS * RING and GROUPS <= P
    REST = E - (GROUPS - 1) * GROUP
    REST_P, REST_J = divmod(REST, J)
    S = D + ED + 1
    BT = 7
    B = BT * P
    BATCHES = TILES // BT
    assert BATCHES * BT == TILES
    BANK = 512
    CUTS = [(0, BANK), (BANK, B)]
    SHIFT = P.bit_length() - 1
    EPS = 1e-5
    DMA = 16

    feats = [x] + [nc.dram_tensor(f"feats_{n}", (NP, D), fp32).ap() for n in range(1, LAYERS)]
    src_groups = src[0:(GROUPS - 1) * GROUP].rearrange("(g p j) -> p g j", p=P, j=J)
    dst_groups = dst[0:(GROUPS - 1) * GROUP].rearrange("(g p j) -> p g j", p=P, j=J)
    attr_groups = edge_attr[0:(GROUPS - 1) * GROUP, :].rearrange("(g p j) c -> g p (j c)", p=P, j=J)

    ctx = ExitStack()
    with ctx:
        def sb(name, shape, dt=fp32):
            return ctx.enter_context(nc.sbuf_tensor(name, shape, dt))

        def pb(name, shape):
            return ctx.enter_context(nc.psum_tensor(name, shape, fp32))

        def sem(name):
            return ctx.enter_context(nc.semaphore(name))

        sums = sb("sums", [S, NP])
        own = sb("own", [S, NP])
        rows = sb("rows", [P, RING, J, S])
        masks = sb("masks", [P, 2, J, P])
        src_all = sb("src_all", [P, GROUPS, J], i32)
        dst_all = sb("dst_all", [P, GROUPS, J], i32)
        dst_f = sb("dst_f", [P, GROUPS, J])
        src_stage = sb("src_stage", [P, RING, J], i32)
        attr_stage = sb("attr_stage", [P, RING, J * ED])
        ident = sb("ident", [P, P])
        iota_sb = sb("iota_sb", [P, P])
        tile_base = sb("tile_base", [P, TILES])
        ends = sb("ends", [P, 2, GROUPS])
        group_ends = sb("group_ends", [P, 2])
        tile_span = sb("tile_span", [1, GROUPS, 2], i32)
        span_nodes = sb("span_nodes", [1, GROUPS, 2], i32)
        w_own = [sb(f"w_own{n}", [S, D]) for n in range(LAYERS)]
        w_sum = [sb(f"w_sum{n}", [S, D]) for n in range(LAYERS)]
        pick_deg = sb("pick_deg", [S, D])
        act_t = sb("act_t", [D, B])
        node_rows = sb("node_rows", [P, 2, BT, D])
        x_rows = sb("x_rows", [P, 2, BT, D])
        sq = sb("sq", [P, BT, D])
        mean = sb("mean", [P, BT])
        var = sb("var", [P, BT])
        std = sb("std", [P, BT])
        rstd = sb("rstd", [P, BT])
        eps = sb("eps", [P, 1])
        zeros = sb("zeros", [D, 1])

        part = pb("part", [P, 2, BANK])
        deg_ps = pb("deg_ps", [P, 2 * BANK])
        conv_ps = pb("conv_ps", [P, 2 * BANK])
        turn_ps = pb("turn_ps", [P, BANK])
        iota_ps = pb("iota_ps", [P, BANK])
        iota = iota_ps[:, 0:P]
        turned = turn_ps[:, 0:BT * D].rearrange("p (t d) -> p t d", d=D)

        def per_node(v):
            return v[:, :].rearrange("p (t a) -> p t a", a=1).to_broadcast([P, BT, D])

        consts_ready = sem("consts_ready")
        zeros_ready = sem("zeros_ready")
        lists_cleared = sem("lists_cleared")
        src_loaded = sem("src_loaded")
        dst_loaded = sem("dst_loaded")
        w_loaded = sem("w_loaded")
        x_loaded = [sem(f"x_loaded{b}") for b in range(2)]
        x_turned = sem("x_turned")
        x_kept = sem("x_kept")
        ends_ready = sem("ends_ready")
        ends_turned = sem("ends_turned")
        group_ends_ready = sem("group_ends_ready")
        group_ends_turned = sem("group_ends_turned")
        span_ready = sem("span_ready")
        src_staged = [sem(f"src_staged{s}") for s in range(RING)]
        rows_landed = [sem(f"rows_landed{s}") for s in range(RING)]
        rows_used = [sem(f"rows_used{s}") for s in range(RING)]
        attr_landed = [sem(f"attr_landed{s}") for s in range(RING)]
        attr_copied = [sem(f"attr_copied{s}") for s in range(RING)]
        masks_ready = sem("masks_ready")
        part_ready = sem("part_ready")
        part_taken = sem("part_taken")
        layer_summed = sem("layer_summed")
        deg_ready = sem("deg_ready")
        own_scaled = sem("own_scaled")
        conv_ready = sem("conv_ready")
        act_ready = sem("act_ready")
        own_kept = sem("own_kept")
        sums_cleared = sem("sums_cleared")
        act_turned = sem("act_turned")
        nodes_ready = sem("nodes_ready")
        nodes_stored = [sem(f"nodes_stored{b}") for b in range(2)]
        dve_step = sem("dve_step")
        norm_step = sem("norm_step")
        var_ready = sem("var_ready")
        std_ready = sem("std_ready")

        handed_back = {"PE": [*rows_used, x_turned, part_ready, act_turned],
                       "DVE": [part_taken, own_kept, nodes_ready],
                       "ACT": [x_kept, act_ready]}

        block = ctx.enter_context(nc.Block())

        @block.sync
        def _(sp):
            sp.wait_ge(lists_cleared, 2)
            last = GROUPS - 1
            for edges, groups, held, loaded in ((src, src_groups, src_all, src_loaded),
                                                (dst, dst_groups, dst_all, dst_loaded)):
                sp.dma_start(held[:, 0:last, :], groups).then_inc(loaded, DMA)
                tail = edges[last * GROUP:last * GROUP + REST_P * J].rearrange("(p j) -> p j", j=J)
                sp.dma_start(held[0:REST_P, last, :], tail).then_inc(loaded, DMA)
                tail = edges[E - REST_J:E].rearrange("(p j) -> p j", p=1)
                sp.dma_start(held[REST_P:REST_P + 1, last, 0:REST_J], tail).then_inc(loaded, DMA)
            for n, (w, b) in enumerate(weights):
                sp.dma_start(w_own[n][0:D, :], w[0:D, :]).then_inc(w_loaded, DMA)
                sp.dma_start(w_sum[n][0:D + ED, :], w[D:2 * D + ED, :]).then_inc(w_loaded, DMA)
                sp.dma_start(w_sum[n][D + ED:S, :], b.rearrange("(a d) -> a d", a=1)).then_inc(w_loaded, DMA)

            def load_x(batch, slot, partial):
                at = batch * B
                count = NODE_REST if partial else P
                sp.dma_start(x_rows[:, slot, 0:BT - 1, :],
                             x[bass.ds(at, (BT - 1) * P), :].rearrange("(t p) d -> p t d", p=P)
                             ).then_inc(x_loaded[slot], DMA)
                sp.dma_start(x_rows[0:count, slot, BT - 1, :],
                             x[bass.ds(at + (BT - 1) * P, count), :]).then_inc(x_loaded[slot], DMA)

            for s in range(RING):
                sp.dma_start(attr_stage[:, s, :], attr_groups[s, :, :]).then_inc(attr_landed[s], DMA)

            for slot in range(2):
                load_x(slot, slot, False)
            with sp.Fori(1, BATCHES // 2 - 1) as i:
                for slot in range(2):
                    sp.wait_ge(x_turned, 2 * i + slot)
                    load_x(2 * i + slot, slot, False)
            for batch in (BATCHES - 2, BATCHES - 1):
                sp.wait_ge(x_turned, batch)
                load_x(batch, batch % 2, batch == BATCHES - 1)

            with sp.Fori(1, ROUNDS - 1) as i:
                for s in range(RING):
                    sp.wait_ge(attr_copied[s], i)
                    sp.dma_start(attr_stage[:, s, :], attr_groups[i * RING + s, :, :]).then_inc(attr_landed[s], DMA)
            for s in range(RING):
                g = (ROUNDS - 1) * RING + s
                sp.wait_ge(attr_copied[s], ROUNDS - 1)
                if g < last:
                    sp.dma_start(attr_stage[:, s, :], attr_groups[g, :, :]).then_inc(attr_landed[s], DMA)
                else:
                    sp.dma_start(attr_stage[0:REST_P, s, :],
                                 edge_attr[last * GROUP:last * GROUP + REST_P * J, :]
                                 .rearrange("(p j) c -> p (j c)", j=J)).then_inc(attr_landed[s], DMA)
                    sp.dma_start(attr_stage[REST_P:REST_P + 1, s, 0:REST_J * ED],
                                 edge_attr[E - REST_J:E, :].rearrange("(p j) c -> p (j c)", p=1)
                                 ).then_inc(attr_landed[s], DMA)

            for layer in range(LAYERS - 1):
                done = layer * BATCHES
                table = feats[layer + 1].rearrange("(b t p) d -> b p t d", p=P, t=BT)
                with sp.Fori(0, BATCHES // 2) as i:
                    for slot in range(2):
                        sp.wait_ge(nodes_ready, 2 * i + (done + slot + 2))
                        sp.dma_start(table[2 * i + slot, :, :, :], node_rows[:, slot, :, :]).then_inc(nodes_stored[slot], DMA)

            done = (LAYERS - 1) * BATCHES

            def store(batch, slot, partial):
                count = NODE_REST if partial else P
                sp.dma_start(out[bass.ds(batch * B, (BT - 1) * P), :].rearrange("(t p) d -> p t d", p=P),
                             node_rows[:, slot, 0:BT - 1, :]).then_inc(nodes_stored[slot], DMA)
                sp.dma_start(out[bass.ds(batch * B + (BT - 1) * P, count), :],
                             node_rows[0:count, slot, BT - 1, :]).then_inc(nodes_stored[slot], DMA)

            for slot in range(2):
                load_x(slot, slot, False)
            with sp.Fori(0, BATCHES // 2 - 2) as i:
                for slot in range(2):
                    sp.wait_ge(nodes_ready, 2 * i + (done + slot + 2))
                    store(2 * i + slot, slot, False)
                    load_x(2 * i + slot + 2, slot, False)
            for batch in range(BATCHES - 4, BATCHES):
                sp.wait_ge(nodes_ready, done + batch + 2)
                store(batch, batch % 2, batch == BATCHES - 1)
                if batch + 2 < BATCHES:
                    load_x(batch + 2, batch % 2, batch + 2 == BATCHES - 1)
            for slot in range(2):
                sp.wait_ge(nodes_stored[slot], DMA * (LAYERS + 1) * BATCHES // 2)

        @block.gpsimd
        def _(pool):
            nc.gpsimd.iota(iota_sb[:, :], pattern=[[1, P]], base=0, channel_multiplier=0,
                           allow_small_or_imprecise_dtypes=True).then_inc(consts_ready, 1)
            nc.gpsimd.iota(tile_base[:, :], pattern=[[P, TILES]], base=0, channel_multiplier=0,
                           allow_small_or_imprecise_dtypes=True).then_inc(consts_ready, 1)
            nc.gpsimd.memset(ident[:, :], 0.0).then_inc(consts_ready, 1)
            nc.gpsimd.memset(pick_deg[:, :], 0.0).then_inc(consts_ready, 1)
            pool.wait_ge(consts_ready, 4)
            nc.gpsimd.affine_select(out=ident[:, :], in_=ident[:, :], compare_op=ALU.not_equal, fill=1.0,
                                    base=0, pattern=[[-1, P]], channel_multiplier=1).then_inc(consts_ready, 1)
            nc.gpsimd.affine_select(out=pick_deg[:, :], in_=pick_deg[:, :], compare_op=ALU.not_equal, fill=1.0,
                                    base=-(S - 1), pattern=[[0, D]], channel_multiplier=1).then_inc(consts_ready, 1)
            for layer in range(LAYERS):
                if layer:
                    for slot in range(2):
                        pool.wait_ge(nodes_stored[slot], DMA * layer * BATCHES // 2)
                with pool.Fori(0, ROUNDS) as i:
                    use = pool.compute_val(i + (layer * ROUNDS + 1))
                    for s in range(RING):
                        pool.wait_ge(src_loaded, 3 * DMA)
                        pool.wait_ge(src_staged[s], use)
                        pool.wait_ge(rows_used[s], use)
                        for j in range(J):
                            nc.gpsimd.indirect_dma_start(
                                rows[:, s, j, 0:D], None, feats[layer],
                                bass.IndirectOffsetOnAxis(ap=src_stage[:, s, j:j + 1], axis=0),
                            ).then_inc(rows_landed[s], DMA)
                if layer < LAYERS - 1:
                    with pool.Fori(0, BATCHES) as b:
                        used = pool.compute_val(b + (layer * BATCHES + 1))
                        pool.wait_ge(zeros_ready, 1)
                        pool.wait_ge(conv_ready, used)
                        nc.gpsimd.tensor_copy(sums[0:D, bass.ds(b * B, B)],
                                              zeros[:, :].to_broadcast([D, B])).then_inc(sums_cleared, 1)

        @block.scalar
        def _(act):
            def stage(layer, i, rest=False):
                for s in range(RING):
                    use = i + layer * ROUNDS
                    if layer or not isinstance(i, int) or i:
                        act.wait_ge(rows_landed[s], use * (J * DMA))
                    nc.scalar.copy(src_stage[:, s, :], src_all[:, i * RING + s, :]).then_inc(src_staged[s], 1)
                    if layer == 0:
                        act.wait_ge(attr_landed[s], (i + 1 + (rest and s == RING - 1)) * DMA)
                        act.wait_ge(rows_used[s], i + 1)
                        nc.scalar.copy(rows[:, s, :, D:D + ED],
                                       attr_stage[:, s, :].rearrange("p (j c) -> p j c", c=ED)
                                       ).then_inc(attr_copied[s], 1)

            for handed in handed_back["ACT"]:
                act.sem_inc(handed, 1)
            act.wait_ge(src_loaded, 3 * DMA)
            stage(0, 0)
            with act.Fori(0, BATCHES) as b:
                act.wait_ge(x_turned, b + 2)
                nc.scalar.copy(own[0:D, bass.ds(b * B, B)], conv_ps[0:D, 0:B]).then_inc(x_kept, 1)
            with act.Fori(1, ROUNDS - 1) as i:
                stage(0, i)
            stage(0, ROUNDS - 1, rest=True)
            for layer in range(LAYERS):
                if layer:
                    with act.Fori(0, ROUNDS) as i:
                        stage(layer, i)
                done = layer * BATCHES
                func = ACT.Relu if layer < LAYERS - 1 else ACT.Copy
                with act.Fori(0, BATCHES) as b:
                    act.wait_ge(conv_ready, b + (done + 1))
                    act.wait_ge(act_turned, b + (done + 1))
                    if layer < LAYERS - 1:
                        act.wait_ge(own_kept, b + (done + 1))
                    nc.scalar.activation(act_t[:, :], conv_ps[0:D, 0:B], func).then_inc(act_ready, 1)
                    if layer == LAYERS - 1:
                        act.wait_ge(var_ready, b + 1)
                        nc.scalar.activation(std[:, :], var[:, :], ACT.Sqrt, bias=eps[:, 0:1],
                                             scale=1.0 / D).then_inc(std_ready, 1)

        @block.vector
        def _(dve):
            steps = [0]

            def ordered(ins):
                ins.then_inc(dve_step, 1)
                steps[0] += 1
                dve.wait_ge(dve_step, steps[0])

            for handed in handed_back["DVE"]:
                dve.sem_inc(handed, 1)
            nc.vector.memset(src_all[:, GROUPS - 1, :], 0).then_inc(lists_cleared, 1)
            nc.vector.memset(dst_all[:, GROUPS - 1, :], NP - 1).then_inc(lists_cleared, 1)
            nc.vector.memset(rows[:, :, :, S - 1:S], 1.0)
            nc.vector.memset(eps[:, :], EPS)
            for w in w_own:
                nc.vector.memset(w[D:S, :], 0.0)
            nc.vector.memset(zeros[:, :], 0.0).then_inc(zeros_ready, 1)
            nc.vector.memset(own[D:S, :], 0.0)
            ordered(nc.vector.memset(sums[:, :], 0.0))
            dve.wait_ge(consts_ready, 6)
            nc.vector.tensor_copy(iota, iota_sb[:, :])
            dve.wait_ge(dst_loaded, 3 * DMA)
            ordered(nc.vector.tensor_copy(dst_f[:, :, :], dst_all[:, :, :]))
            nc.vector.tensor_reduce(ends[:, 0, :], dst_f[:, :, :], axis=X, op=ALU.min)
            nc.vector.tensor_reduce(ends[:, 1, :], dst_f[:, :, :], axis=X, op=ALU.max).then_inc(ends_ready, 1)
            dve.wait_ge(ends_turned, 1)
            nc.vector.tensor_reduce(group_ends[0:GROUPS, 0:1], deg_ps[0:GROUPS, 0:P], axis=X, op=ALU.min)
            nc.vector.tensor_reduce(group_ends[0:GROUPS, 1:2], deg_ps[0:GROUPS, P:2 * P], axis=X,
                                    op=ALU.max).then_inc(group_ends_ready, 1)
            dve.wait_ge(group_ends_turned, 1)
            ordered(nc.vector.tensor_copy(span_nodes[:, :, :],
                                          deg_ps[0:1, BANK:BANK + 2 * GROUPS].rearrange("p (e g) -> p g e", e=2)))
            nc.vector.tensor_scalar(tile_span[:, :, :], span_nodes[:, :, :], SHIFT, None,
                                    ALU.arith_shift_right).then_inc(span_ready, 1)
            dve.wait_ge(span_ready, 1)

            pairs = dve.alloc_register("dve_pairs")
            before = dve.alloc_register("dve_before")
            dve.reg_mov(pairs, 0)
            for layer in range(LAYERS):
                width = S if layer == 0 else D

                def take_part(k, t):
                    dve.wait_ge(part_ready, k + 1)
                    dve.wait_ge(part_taken, k + 1)
                    here = sums[0:width, bass.ds(t * P, P)]
                    return nc.vector.tensor_tensor(here, part[0:width, (k + 1) % 2, 0:P], here, ALU.add)

                ordered(nc.vector.memset(part[:, :, 0:P], 0.0))
                dve.reg_mov(before, 0)
                if layer:
                    dve.wait_ge(sums_cleared, layer * BATCHES)
                with dve.Fori(0, GROUPS) as g:
                    first = dve.value_load(tile_span[0:1, g, 0:1], min_val=0, max_val=TILES - 1)
                    last = dve.value_load(tile_span[0:1, g, 1:2], min_val=0, max_val=TILES - 1)
                    with dve.Fori(first, last + 1) as t:
                        k = dve.snap(pairs, min_val=0, max_val=LAYERS * GROUPS * TILES)
                        nc.vector.scalar_tensor_tensor(
                            out=masks[:, k % 2, :, :],
                            in0=dst_f[:, g, :].rearrange("p (j a) -> p j a", a=1).to_broadcast([P, J, P]),
                            scalar=tile_base[:, bass.ds(t, 1)],
                            in1=iota.rearrange("p (a n) -> p a n", a=1).to_broadcast([P, J, P]),
                            op0=ALU.subtract, op1=ALU.is_equal).then_inc(masks_ready, 1)
                        take_part(k, dve.snap(before, min_val=0, max_val=TILES - 1)).then_inc(part_taken, 1)
                        dve.reg_mov(before, t)
                        dve.reg_add(pairs, pairs, 1)
                take_part(dve.snap(pairs, min_val=0, max_val=LAYERS * GROUPS * TILES),
                          dve.snap(before, min_val=0, max_val=TILES - 1)).then_inc(layer_summed, 1)
                done = layer * BATCHES
                def node_batches(i):
                    for slot in range(2):
                        n = 2 * i + slot
                        here = own[0:D, bass.ds(n * B, B)]
                        if layer == 0:
                            dve.wait_ge(deg_ready, n + 1)
                            dve.wait_ge(x_kept, BATCHES + 1)
                            nc.vector.tensor_tensor(here, deg_ps[0:D, 0:B], here, ALU.mult).then_inc(own_scaled, 1)
                        if layer < LAYERS - 1:
                            dve.wait_ge(act_ready, n + (done + 2))
                            dve.wait_ge(deg_ready, n + (done + 1))
                            nc.vector.tensor_tensor(here, deg_ps[0:D, 0:B], act_t[:, :],
                                                    ALU.mult).then_inc(own_kept, 1)
                            dve.wait_ge(act_turned, n + (done + 2))
                            if layer or not isinstance(i, int):
                                dve.wait_ge(nodes_stored[slot], (i + layer * BATCHES // 2) * DMA)
                            nc.vector.tensor_copy(node_rows[:, slot, :, :], turned).then_inc(nodes_ready, 1)
                        else:
                            def ordered_norm(ins, step):
                                ins.then_inc(norm_step, 1)
                                dve.wait_ge(norm_step, n * 5 + step)

                            z = node_rows[:, slot, :, :]
                            dve.wait_ge(act_turned, n + (done + 2))
                            dve.wait_ge(x_loaded[slot], (i + (BATCHES // 2 + 1)) * 2 * DMA)
                            dve.wait_ge(nodes_stored[slot], (i * 2 + layer * BATCHES // 2) * DMA)
                            ordered_norm(nc.vector.tensor_tensor(z, turned, x_rows[:, slot, :, :], ALU.add), 1)
                            ordered_norm(nc.vector.tensor_reduce(mean[:, :], z, axis=X, op=ALU.add), 2)
                            ordered_norm(nc.vector.scalar_tensor_tensor(
                                out=z, in0=per_node(mean), scalar=-1.0 / D, in1=z, op0=ALU.mult, op1=ALU.add), 3)
                            ordered_norm(nc.vector.tensor_tensor(sq[:, :, :], z, z, ALU.mult), 4)
                            nc.vector.tensor_reduce(var[:, :], sq[:, :, :], axis=X, op=ALU.add).then_inc(var_ready, 1)
                            dve.wait_ge(std_ready, n + 1)
                            ordered_norm(nc.vector.reciprocal(rstd[:, :], std[:, :]), 5)
                            nc.vector.tensor_tensor(z, z, per_node(rstd), ALU.mult).then_inc(nodes_ready, 1)

                if layer == 0:
                    node_batches(0)
                    with dve.Fori(1, BATCHES // 2) as i:
                        node_batches(i)
                else:
                    with dve.Fori(0, BATCHES // 2) as i:
                        node_batches(i)

        @block.tensor
        def _(pe):
            for handed in handed_back["PE"]:
                pe.sem_inc(handed, 1)
            pe.wait_ge(consts_ready, 6)
            pe.wait_ge(ends_ready, 1)
            nc.tensor.transpose(deg_ps[0:GROUPS, 0:P], ends[:, 0, :], ident[:, :])
            nc.tensor.transpose(deg_ps[0:GROUPS, P:2 * P], ends[:, 1, :], ident[:, :]).then_inc(ends_turned, 1)
            pe.wait_ge(group_ends_ready, 1)
            for e in range(2):
                last = nc.tensor.transpose(deg_ps[0:1, BANK + e * GROUPS:BANK + (e + 1) * GROUPS],
                                           group_ends[0:GROUPS, e:e + 1], ident[0:GROUPS, 0:GROUPS])
            last.then_inc(group_ends_turned, 1)
            with pe.Fori(0, BATCHES // 2) as i:
                for slot in range(2):
                    kept = pe.compute_val(2 * i + (slot + 1))
                    loaded = pe.compute_val((i + 1) * 2 * DMA)
                    pe.wait_ge(consts_ready, 6)
                    pe.wait_ge(x_loaded[slot], loaded)
                    pe.wait_ge(x_kept, kept)
                    for t in range(BT):
                        last = nc.tensor.transpose(conv_ps[0:D, t * P:(t + 1) * P], x_rows[:, slot, t, :], ident[:, :])
                    last.then_inc(x_turned, 1)

            pe.wait_ge(span_ready, 1)
            pe.wait_ge(w_loaded, 3 * LAYERS * DMA)
            pairs = pe.alloc_register("pe_pairs")
            pe.reg_mov(pairs, 0)
            for layer in range(LAYERS):
                width = S if layer == 0 else D
                with pe.Fori(0, ROUNDS) as i:
                    landed = pe.compute_val((i + (1 + layer * ROUNDS)) * (J * DMA))
                    copied = pe.compute_val(i + 1)
                    for s in range(RING):
                        g = i * RING + s
                        first = pe.value_load(tile_span[0:1, g, 0:1], min_val=0, max_val=TILES - 1)
                        last = pe.value_load(tile_span[0:1, g, 1:2], min_val=0, max_val=TILES - 1)
                        pe.wait_ge(span_ready, 1)
                        pe.wait_ge(rows_landed[s], landed)
                        if layer == 0:
                            pe.wait_ge(attr_copied[s], copied)
                        with pe.Fori(first, last + 1) as t:
                            k = pe.snap(pairs, min_val=0, max_val=LAYERS * GROUPS * TILES)
                            pe.wait_ge(masks_ready, k + 1)
                            pe.wait_ge(part_taken, k + 1)
                            for j in range(J):
                                mm = nc.tensor.matmul(part[0:width, k % 2, 0:P], rows[:, s, j, 0:width],
                                                      masks[:, k % 2, j, :], start=(j == 0), stop=(j == J - 1))
                            mm.then_inc(part_ready, 1)
                            pe.reg_add(pairs, pairs, 1)
                        pe.drain().then_inc(rows_used[s], 1)

                done = layer * BATCHES
                pe.wait_ge(layer_summed, layer + 1)
                if layer:
                    pe.wait_ge(own_kept, done + 1)
                with pe.Fori(0, BATCHES) as b:
                    handed = pe.compute_val(b + (done + 1))
                    made = pe.compute_val(b + (done + 2))
                    if layer < LAYERS - 1:
                        pe.wait_ge(own_kept, handed)
                        for lo, hi in CUTS:
                            last = nc.tensor.matmul(deg_ps[0:D, lo:hi], pick_deg[:, :],
                                                    sums[:, bass.ds(b * B + lo, hi - lo)], start=True, stop=True)
                        last.then_inc(deg_ready, 1)
                    if layer == 0:
                        pe.wait_ge(own_scaled, b + 1)
                    pe.wait_ge(act_ready, handed)
                    for lo, hi in CUTS:
                        nc.tensor.matmul(conv_ps[0:D, lo:hi], w_own[layer][:, :],
                                         own[:, bass.ds(b * B + lo, hi - lo)], start=True, stop=False)
                        last = nc.tensor.matmul(conv_ps[0:D, lo:hi], w_sum[layer][:, :],
                                                sums[:, bass.ds(b * B + lo, hi - lo)], start=False, stop=True)
                    last.then_inc(conv_ready, 1)
                    pe.wait_ge(consts_ready, 6)
                    pe.wait_ge(act_ready, made)
                    pe.wait_ge(nodes_ready, handed)
                    for t in range(BT):
                        last = nc.tensor.transpose(turn_ps[:, t * D:(t + 1) * D], act_t[:, t * P:(t + 1) * P],
                                                   ident[0:D, 0:D])
                    last.then_inc(act_turned, 1)


_INS = ["x", "src", "dst", "edge_attr_16", "L0_gnn_W1", "L0_gnn_b1", "L0_gnn_W2", "L0_gnn_b2",
        "L0_gnn_W3", "L0_gnn_b3"]


def kernel(**inputs):
    import numpy as _np
    import concourse.bacc as _bacc
    from concourse import mybir as _mybir
    from concourse.bass_utils import run_bass_kernel_spmd as _run

    nc = _bacc.Bacc("TRN2", target_bir_lowering=False, num_devices=1)
    arrays, aps = {}, {}
    for name in _INS:
        a = _np.ascontiguousarray(inputs[name])
        arrays[f"in_{name}"] = a
        aps[name] = nc.dram_tensor(f"in_{name}", a.shape, _mybir.dt.from_np(a.dtype), kind="ExternalInput").ap()
    out = nc.dram_tensor("out_0", inputs["x"].shape, _mybir.dt.float32, kind="ExternalOutput").ap()
    weights = [(aps[f"L0_gnn_W{n}"], aps[f"L0_gnn_b{n}"]) for n in (1, 2, 3)]
    gnn_kernel(nc, aps["x"], aps["src"], aps["dst"], aps["edge_attr_16"], weights, out)
    r = _run(nc, [arrays], core_ids=[0])
    return r.results[0]["out_0"]
```

```python
import concourse.bass as bass
from concourse import mybir
from contextlib import ExitStack


def gnn_kernel(nc, x, src, dst, edge_attr, weights, out):
    fp32 = mybir.dt.float32
    bf16 = mybir.dt.bfloat16
    fp16 = mybir.dt.float16
    i32 = mybir.dt.int32
    ALU = mybir.AluOpType
    ACT = mybir.ActivationFunctionType
    X = mybir.AxisListType.X

    N, D = x.shape
    E, ED = edge_attr.shape
    P = nc.NUM_PARTITIONS
    LAYERS = len(weights)
    TILES = -(-N // P)
    NP = TILES * P
    NODE_REST = N - (TILES - 1) * P
    J = 11
    W = 11
    SLOTS = J * W
    GROUP = P * J
    RING = 4
    ALL_GROUPS = -(-E // GROUP)
    ROUNDS0 = -(-ALL_GROUPS // RING)
    GROUPS = ROUNDS0 * RING
    PER_ROUND = 3
    CROUNDS = 21
    COUNTED = PER_ROUND * CROUNDS
    ROUNDS = (ALL_GROUPS - COUNTED) // RING
    assert COUNTED + ROUNDS * RING == ALL_GROUPS and CROUNDS <= ROUNDS
    assert ALL_GROUPS > P >= GROUPS - P
    LAST = ALL_GROUPS - 1
    REST = E - LAST * GROUP
    REST_P, REST_J = divmod(REST, J)
    S = D + ED + 1
    PARTS = 3
    HALF = 50
    BPER_ROUND = 2
    BROUNDS, BREST = divmod(COUNTED, BPER_ROUND)
    assert BREST == 1 and BROUNDS + 1 < ROUNDS0
    BRING = 2
    HALVES = [range(0, HALF), range(HALF, TILES)]
    BANK = 512
    QUARTER = HALF // 2 * W
    CRING = 3
    BT = 7
    B = BT * P
    BATCHES = TILES // BT
    assert BATCHES * BT == TILES and QUARTER <= BANK and SLOTS <= P
    CUTS = [(0, BANK), (BANK, B)]
    SHIFT = P.bit_length() - 1
    EPS = 1e-5
    DMA = 16
    USES = [0] + [ROUNDS0 + ROUNDS * n for n in range(LAYERS)]
    MAX_PAIRS = LAYERS * 2 * GROUPS * TILES

    feats = [x] + [nc.dram_tensor(f"feats_{n}", (NP, D), fp32).ap() for n in range(1, LAYERS)]
    own_t = [None] + [nc.dram_tensor(f"own_t_{n}", (D, NP), fp32).ap() for n in range(1, LAYERS)]
    counts = nc.dram_tensor("counts", (COUNTED, 2, P, HALF * SLOTS), bf16).ap()
    src_groups = src[0:LAST * GROUP].rearrange("(g p j) -> p g j", p=P, j=J)
    dst_groups = dst[0:LAST * GROUP].rearrange("(g p j) -> p g j", p=P, j=J)
    attr_groups = edge_attr[0:LAST * GROUP, :].rearrange("(g p j) c -> g p (j c)", p=P, j=J)

    ctx = ExitStack()
    with ctx:
        def sb(name, shape, dt=fp32):
            return ctx.enter_context(nc.sbuf_tensor(name, shape, dt))

        def pb(name, shape):
            return ctx.enter_context(nc.psum_tensor(name, shape, fp32))

        def sem(name):
            return ctx.enter_context(nc.semaphore(name))

        sums = sb("sums", [S, NP + P])
        rows = sb("rows", [P, RING, J, S])
        masks = sb("masks", [P, 2, J, P])
        src_all = sb("src_all", [P, GROUPS, J], i32)
        dst_rel = sb("dst_rel", [P, GROUPS, J])
        src_stage = sb("src_stage", [P, RING, J], i32)
        attr_stage = sb("attr_stage", [P, RING, J * ED])
        ident = sb("ident", [P, P])
        iota_sb = sb("iota_sb", [P, P])
        from_one = sb("from_one", [P, 2 * HALF * W], fp16)
        window_base = sb("window_base", [P, TILES])
        ends = sb("ends", [P, 2, GROUPS])
        group_ends = sb("group_ends", [P, 2, 2])
        span = sb("span", [1, GROUPS, 2], i32)
        w_own = [sb(f"w_own{n}", [D, D]) for n in range(LAYERS)]
        w_sum = [sb(f"w_sum{n}", [S, D]) for n in range(LAYERS)]
        pick_deg = sb("pick_deg", [S, D])

        parts = sb("parts", [P, TILES, PARTS, D], bf16)
        blocks_flat = sb("blocks", [P, CRING * HALF * SLOTS], bf16)
        blocks = blocks_flat[:, :].rearrange("p (r h s) -> p r h s", r=CRING, h=HALF)
        is_low = sb("is_low", [P, 2, P], bf16)
        is_key = sb("is_key", [P, 2, HALF * W], bf16)
        keys = sb("keys", [P, 2, J, COUNTED])
        least = sb("least", [COUNTED, J])
        reach = sb("reach", [COUNTED, 1])
        narrow = sb("narrow", [COUNTED, 1])
        wide = sb("wide", [COUNTED, 1])
        slot_iota = sb("slot_iota", [COUNTED, J, W])
        slot_rows = sb("slot_rows", [COUNTED, J, W])
        slot_node = sb("slot_node", [SLOTS, COUNTED])
        wide_row = sb("wide_row", [1, COUNTED], i32)
        any_wide_f = sb("any_wide_f", [1, 1])
        any_wide = sb("any_wide", [1, 1], i32)
        slot_sums = sb("slot_sums", [SLOTS, D])

        own = sb("own", [D, 2, B])
        act_t = sb("act_t", [D, B])
        node_rows = sb("node_rows", [P, 2, BT, D])
        x_rows = sb("x_rows", [P, 2, BT, D])
        left = sb("left", [P, BT, D])
        mean = sb("mean", [P, BT])
        var = sb("var", [P, BT])
        std = sb("std", [P, BT])
        rstd = sb("rstd", [P, BT])
        eps = sb("eps", [P, 1])
        zeros = sb("zeros", [D, 1])
        blank = sb("blank", [P, 1], bf16)

        early = blocks_flat[:, :].bitcast(i32)
        dst_all = early[:, 0:GROUPS * J].rearrange("p (g j) -> p g j", j=J)
        early = parts[0:COUNTED, :, :, :].rearrange("p t k d -> p (t k d)").bitcast(i32)

        def early_list(n):
            return early[:, n * GROUP:(n + 1) * GROUP].rearrange("g (c e) -> g c e", c=J)

        chunk_dst, chunk_src, chunk_tile, chunk_low = (early_list(n) for n in range(4))
        chunk_off, chunk_key = (early_list(n).bitcast(fp32) for n in range(4, 6))
        chunk_low_f = chunk_dst.bitcast(fp32)

        part = pb("part", [P, 2, BANK])
        build = pb("build", [P, 4, BANK])
        turn_ps = pb("turn_ps", [P, BANK])
        iota_ps = pb("iota_ps", [P, BANK])
        iota = iota_ps[:, 0:P]
        base_ps = build[:, 3, P:P + GROUPS]
        deg_ps = build[:, 0:2, :].rearrange("p b c -> p (b c)")
        conv_ps = build[:, 2:4, :].rearrange("p b c -> p (b c)")
        x_ps = part[:, :, :].rearrange("p b c -> p (b c)")
        slots_ps = turn_ps[0:SLOTS, 0:PARTS * D]
        turned = turn_ps[:, 0:BT * D].rearrange("p (t d) -> p t d", d=D)

        def per_node(v):
            return v[:, :].rearrange("p (t a) -> p t a", a=1).to_broadcast([P, BT, D])

        consts_ready = sem("consts_ready")
        lists_cleared = sem("lists_cleared")
        src_loaded = sem("src_loaded")
        dst_loaded = sem("dst_loaded")
        chunks_loaded = sem("chunks_loaded")
        w_loaded = sem("w_loaded")
        ends_ready = sem("ends_ready")
        ends_turned = sem("ends_turned")
        group_ends_ready = sem("group_ends_ready")
        group_ends_turned = sem("group_ends_turned")
        keys_made = sem("keys_made")
        keys_turned = sem("keys_turned")
        lists_ready = sem("lists_ready")
        src_staged = [sem(f"src_staged{s}") for s in range(RING)]
        rows_landed = [sem(f"rows_landed{s}") for s in range(RING)]
        rows_used = [sem(f"rows_used{s}") for s in range(RING)]
        attr_landed = [sem(f"attr_landed{s}") for s in range(RING)]
        attr_copied = [sem(f"attr_copied{s}") for s in range(RING)]
        masks_ready = sem("masks_ready")
        part_ready = sem("part_ready")
        part_taken = sem("part_taken")
        onehots_ready = sem("onehots_ready")
        chunk_built = sem("chunk_built")
        chunk_kept = sem("chunk_kept")
        block_stored = [sem(f"block_stored{r}") for r in range(BRING)]
        block_loaded = [sem(f"block_loaded{r}") for r in range(CRING)]
        block_used = [sem(f"block_used{r}") for r in range(CRING)]
        slots_summed = sem("slots_summed")
        slots_taken = sem("slots_taken")
        wide_staged = sem("wide_staged")
        wide_landed = sem("wide_landed")
        wide_used = sem("wide_used")
        layer_summed = sem("layer_summed")
        deg_ready = sem("deg_ready")
        x_loaded = [sem(f"x_loaded{b}") for b in range(2)]
        x_turned = sem("x_turned")
        x_kept = sem("x_kept")
        own_loaded = [sem(f"own_loaded{b}") for b in range(2)]
        own_scaled = sem("own_scaled")
        conv_ready = sem("conv_ready")
        act_ready = sem("act_ready")
        own_kept = sem("own_kept")
        own_stored = [sem(f"own_stored{b}") for b in range(2)]
        sums_cleared = sem("sums_cleared")
        act_turned = sem("act_turned")
        nodes_ready = sem("nodes_ready")
        nodes_stored = [sem(f"nodes_stored{b}") for b in range(2)]
        dve_step = sem("dve_step")
        split_step = sem("split_step")
        norm_step = sem("norm_step")
        var_ready = sem("var_ready")
        std_ready = sem("std_ready")

        handed_back = {"PE": [*rows_used, *block_used, part_ready, x_turned, act_turned, wide_used],
                       "DVE": [part_taken, own_kept, nodes_ready, slots_taken],
                       "ACT": [act_ready]}

        block = ctx.enter_context(nc.Block())

        @block.sync
        def _(sp):
            sp.wait_ge(lists_cleared, 2)
            for edges, groups, held, loaded in ((src, src_groups, src_all, src_loaded),
                                                (dst, dst_groups, dst_all, dst_loaded)):
                sp.dma_start(held[:, 0:LAST, :], groups).then_inc(loaded, DMA)
                tail = edges[LAST * GROUP:LAST * GROUP + REST_P * J].rearrange("(p j) -> p j", j=J)
                sp.dma_start(held[0:REST_P, LAST, :], tail).then_inc(loaded, DMA)
                tail = edges[E - REST_J:E].rearrange("(p j) -> p j", p=1)
                sp.dma_start(held[REST_P:REST_P + 1, LAST, 0:REST_J], tail).then_inc(loaded, DMA)
            for edges, held in ((dst, chunk_dst), (src, chunk_src)):
                sp.dma_start(held, edges[0:COUNTED * GROUP].rearrange("(g c e) -> g c e", c=J, e=P)
                             ).then_inc(chunks_loaded, DMA)

            def load_attr(i, s):
                g = i * RING + s
                if not isinstance(i, int) or g < LAST:
                    sp.dma_start(attr_stage[:, s, :], attr_groups[g, :, :]).then_inc(attr_landed[s], DMA)
                elif g == LAST:
                    sp.dma_start(attr_stage[0:REST_P, s, :],
                                 edge_attr[LAST * GROUP:LAST * GROUP + REST_P * J, :]
                                 .rearrange("(p j) c -> p (j c)", j=J)).then_inc(attr_landed[s], DMA)
                    sp.dma_start(attr_stage[REST_P:REST_P + 1, s, 0:REST_J * ED],
                                 edge_attr[E - REST_J:E, :].rearrange("(p j) c -> p (j c)", p=1)
                                 ).then_inc(attr_landed[s], DMA)

            for s in range(RING):
                load_attr(0, s)
            for n, (w, b) in enumerate(weights):
                sp.dma_start(w_own[n][:, :], w[0:D, :]).then_inc(w_loaded, DMA)
                sp.dma_start(w_sum[n][0:D + ED, :], w[D:2 * D + ED, :]).then_inc(w_loaded, DMA)
                sp.dma_start(w_sum[n][D + ED:S, :], b.rearrange("(a d) -> a d", a=1)).then_inc(w_loaded, DMA)

            def store_half(i, h):
                sp.wait_ge(chunk_kept, (i * RING + (h + 1)) * J)
                sp.dma_start(counts[i * BPER_ROUND + h // 2, h % 2, :, :],
                             blocks[:, h % BRING, :, :].rearrange("p h s -> p (h s)")
                             ).then_inc(block_stored[h % BRING], DMA)

            def first_round(i, halves):
                for s in range(RING):
                    sp.wait_ge(attr_copied[s], i + 1)
                    load_attr(i + 1, s)
                    if s < halves:
                        store_half(i, s)

            with sp.Fori(0, BROUNDS) as i:
                first_round(i, RING)
            first_round(BROUNDS, 2 * BREST)
            with sp.Fori(BROUNDS + 1, ROUNDS0 - 2) as i:
                first_round(i, 0)
            for s in range(RING):
                sp.wait_ge(attr_copied[s], ROUNDS0 - 1)
                load_attr(ROUNDS0 - 1, s)

            def load_x(batch, slot):
                last = isinstance(batch, int) and batch == BATCHES - 1
                count = NODE_REST if last else P
                sp.dma_start(x_rows[:, slot, 0:BT - 1, :],
                             x[bass.ds(batch * B, (BT - 1) * P), :].rearrange("(t p) d -> p t d", p=P)
                             ).then_inc(x_loaded[slot], DMA)
                sp.dma_start(x_rows[0:count, slot, BT - 1, :],
                             x[bass.ds(batch * B + (BT - 1) * P, count), :]).then_inc(x_loaded[slot], DMA)

            def load_own(layer, batch, slot):
                sp.dma_start(own[:, slot, :], own_t[layer][:, bass.ds(batch * B, B)]).then_inc(own_loaded[slot], DMA)

            def store_out(batch, slot):
                last = isinstance(batch, int) and batch == BATCHES - 1
                count = NODE_REST if last else P
                sp.dma_start(out[bass.ds(batch * B, (BT - 1) * P), :].rearrange("(t p) d -> p t d", p=P),
                             node_rows[:, slot, 0:BT - 1, :]).then_inc(nodes_stored[slot], DMA)
                sp.dma_start(out[bass.ds(batch * B + (BT - 1) * P, count), :],
                             node_rows[0:count, slot, BT - 1, :]).then_inc(nodes_stored[slot], DMA)

            def node_batch(layer, i, slot, ahead):
                batch = 2 * i + slot
                done = layer * BATCHES
                if layer < LAYERS - 1:
                    sp.wait_ge(own_kept, 2 * i + (done + slot + 2))
                    sp.dma_start(own_t[layer + 1][:, bass.ds(batch * B, B)], own[:, slot, :]).then_inc(own_stored[slot], DMA)
                    table = feats[layer + 1].rearrange("(b t p) d -> b p t d", p=P, t=BT)
                    sp.wait_ge(nodes_ready, 2 * i + (done + slot + 2))
                    sp.dma_start(table[batch, :, :, :], node_rows[:, slot, :, :]).then_inc(nodes_stored[slot], DMA)
                else:
                    sp.wait_ge(nodes_ready, 2 * i + (done + slot + 2))
                    store_out(batch, slot)
                if ahead:
                    if layer:
                        if layer < LAYERS - 1:
                            sp.wait_ge(own_stored[slot], (i + (layer * BATCHES // 2 + 1)) * DMA)
                        load_own(layer, batch + 2, slot)
                    if layer in (0, LAYERS - 1):
                        load_x(batch + 2, slot)

            for layer in range(LAYERS):
                if layer:
                    if layer == 1:
                        for r in range(BRING):
                            sp.wait_ge(block_stored[r], COUNTED * 2 // BRING * DMA)
                    for slot in range(2):
                        sp.wait_ge(own_stored[slot], layer * BATCHES // 2 * DMA)
                    with sp.Fori(0, CROUNDS) as i:
                        for h in range(2 * PER_ROUND):
                            r = h % CRING
                            use = i * 2 + ((layer - 1) * CROUNDS * 2 + h // CRING)
                            sp.wait_ge(block_used[r], use + 1)
                            sp.dma_start(blocks[:, r, :, :].rearrange("p h s -> p (h s)"),
                                         counts[i * PER_ROUND + h // 2, h % 2, :, :]).then_inc(block_loaded[r], DMA)
                for slot in range(2):
                    if layer:
                        load_own(layer, slot, slot)
                    if layer in (0, LAYERS - 1):
                        load_x(slot, slot)
                with sp.Fori(0, BATCHES // 2 - 2) as i:
                    for slot in range(2):
                        node_batch(layer, i, slot, True)
                for i in range(BATCHES // 2 - 2, BATCHES // 2):
                    for slot in range(2):
                        node_batch(layer, i, slot, i < BATCHES // 2 - 1)
            for slot in range(2):
                sp.wait_ge(nodes_stored[slot], DMA * (LAYERS + 1) * BATCHES // 2)

        @block.gpsimd
        def _(pool):
            nc.gpsimd.iota(iota_sb[:, :], pattern=[[1, P]], base=0, channel_multiplier=0,
                           allow_small_or_imprecise_dtypes=True).then_inc(consts_ready, 1)
            nc.gpsimd.iota(window_base[:, :], pattern=[[P, TILES]], base=0, channel_multiplier=0,
                           allow_small_or_imprecise_dtypes=True).then_inc(consts_ready, 1)
            nc.gpsimd.iota(from_one[:, :], pattern=[[1, 2 * HALF * W]], base=1, channel_multiplier=0,
                           allow_small_or_imprecise_dtypes=True).then_inc(consts_ready, 1)
            nc.gpsimd.iota(slot_iota[:, :, :], pattern=[[0, J], [1, W]], base=0, channel_multiplier=0,
                           allow_small_or_imprecise_dtypes=True).then_inc(consts_ready, 1)
            nc.gpsimd.memset(ident[:, :], 0.0).then_inc(consts_ready, 1)
            nc.gpsimd.memset(pick_deg[:, :], 0.0).then_inc(consts_ready, 1)
            pool.wait_ge(consts_ready, 6)
            nc.gpsimd.affine_select(out=ident[:, :], in_=ident[:, :], compare_op=ALU.not_equal, fill=1.0,
                                    base=0, pattern=[[-1, P]], channel_multiplier=1).then_inc(consts_ready, 1)
            nc.gpsimd.affine_select(out=pick_deg[:, :], in_=pick_deg[:, :], compare_op=ALU.not_equal, fill=1.0,
                                    base=-(S - 1), pattern=[[0, D]], channel_multiplier=1).then_inc(consts_ready, 1)

            def gather(layer, s, landed):
                for j in range(J):
                    nc.gpsimd.indirect_dma_start(
                        rows[:, s, j, 0:D], None, feats[layer],
                        bass.IndirectOffsetOnAxis(ap=src_stage[:, s, j:j + 1], axis=0),
                    ).then_inc(landed, DMA)

            wides = pool.alloc_register("pool_wides")
            pool.reg_mov(wides, 0)
            for layer in range(LAYERS):
                if layer:
                    for slot in range(2):
                        pool.wait_ge(nodes_stored[slot], DMA * layer * BATCHES // 2)
                with pool.Fori(0, ROUNDS if layer else ROUNDS0) as i:
                    use = pool.compute_val(i + (USES[layer] + 1))
                    for s in range(RING):
                        pool.wait_ge(src_loaded, 3 * DMA)
                        pool.wait_ge(src_staged[s], use)
                        pool.wait_ge(rows_used[s], use)
                        gather(layer, s, rows_landed[s])
                if layer:
                    pool.wait_ge(lists_ready, 1)
                    pool.wait_ge(rows_used[0], USES[layer + 1] + 1)
                    some = pool.value_load(any_wide[0:1, 0:1], min_val=0, max_val=1)
                    with pool.If(some > 0):
                        with pool.Fori(0, COUNTED) as g:
                            is_wide = pool.value_load(wide_row[0:1, bass.ds(g, 1)], min_val=0, max_val=1)
                            with pool.If(is_wide > 0):
                                count = pool.snap(wides, min_val=0, max_val=LAYERS * COUNTED)
                                use = pool.compute_val(count + 1)
                                pool.wait_ge(wide_used, use)
                                nc.gpsimd.tensor_copy(src_stage[:, 0, :], src_all[:, g, :]).then_inc(wide_staged, 1)
                                pool.wait_ge(src_loaded, 3 * DMA)
                                pool.wait_ge(wide_staged, use)
                                gather(layer, 0, wide_landed)
                                pool.reg_add(wides, wides, 1)
                if layer < LAYERS - 1:
                    with pool.Fori(0, BATCHES) as b:
                        used = pool.compute_val(b + (layer * BATCHES + 1))
                        pool.wait_ge(consts_ready, 8)
                        pool.wait_ge(conv_ready, used)
                        nc.gpsimd.tensor_copy(sums[0:D, bass.ds(b * B, B)],
                                              zeros[:, :].to_broadcast([D, B])).then_inc(sums_cleared, 1)

        @block.scalar
        def _(act):
            for handed in handed_back["ACT"]:
                act.sem_inc(handed, 1)

            def stage(layer, i, s, first_group):
                if layer or not isinstance(i, int) or i:
                    act.wait_ge(rows_landed[s], (i + USES[layer]) * (J * DMA))
                nc.scalar.copy(src_stage[:, s, :], src_all[:, i * RING + (first_group + s), :]).then_inc(src_staged[s], 1)

            def place_attr(i, s):
                g = i * RING + s
                static = isinstance(i, int)
                loads = i + 1 if not static or g < LAST else i + 2 if g == LAST else i
                act.wait_ge(attr_landed[s], loads * DMA)
                act.wait_ge(rows_used[s], i + 1)
                nc.scalar.copy(rows[:, s, :, D:D + ED],
                               attr_stage[:, s, :].rearrange("p (j c) -> p j c", c=ED)
                               ).then_inc(attr_copied[s], 1)

            def keep_half(i, h):
                r = h % BRING
                if not isinstance(i, int) or i or h >= BRING:
                    act.wait_ge(block_stored[r], (i * (RING // BRING) + h // BRING) * DMA)
                for c in range(J):
                    n = i * (RING * J) + (h * J + c)
                    act.wait_ge(chunk_built, n + 1)
                    pair = (h * J + c) % 2
                    nc.scalar.copy(
                        blocks[:, r, :, c * W:(c + 1) * W].rearrange("p (b t) w -> p b t w", b=2),
                        build[:, 2 * pair:2 * pair + 2, 0:QUARTER].rearrange("p b (t w) -> p b t w", w=W),
                    ).then_inc(chunk_kept, 1)

            def first_round(i, halves, more=True):
                for s in range(RING):
                    if s == 0:
                        stage(0, i, RING - 1, 0)
                    elif more:
                        stage(0, i + 1, s - 1, 0)
                    if s < RING - 1:
                        place_attr(i, s + 1)
                    elif more:
                        place_attr(i + 1, 0)
                    if s < halves:
                        keep_half(i, s)

            act.wait_ge(src_loaded, 3 * DMA)
            for s in range(RING - 1):
                stage(0, 0, s, 0)
            place_attr(0, 0)
            first_round(0, RING)
            with act.Fori(1, BROUNDS) as i:
                first_round(i, RING)
            first_round(BROUNDS, 2 * BREST)
            with act.Fori(BROUNDS + 1, ROUNDS0 - 1) as i:
                first_round(i, 0)
            first_round(ROUNDS0 - 1, 0, more=False)

            def node_batch(layer, i, slot):
                done = layer * BATCHES
                b = 2 * i + slot
                if layer == 0:
                    act.wait_ge(x_turned, b + 2)
                    if not isinstance(i, int) or i:
                        act.wait_ge(own_stored[slot], i * DMA)
                    nc.scalar.copy(own[:, slot, :], x_ps[0:D, 0:B]).then_inc(x_kept, 1)
                act.wait_ge(conv_ready, b + (done + 1))
                act.wait_ge(act_turned, b + (done + 1))
                if layer < LAYERS - 1:
                    act.wait_ge(own_kept, b + (done + 1))
                nc.scalar.activation(act_t[:, :], conv_ps[0:D, 0:B],
                                     ACT.Relu if layer < LAYERS - 1 else ACT.Copy).then_inc(act_ready, 1)
                if layer == LAYERS - 1:
                    act.wait_ge(var_ready, b + 1)
                    nc.scalar.activation(std[:, :], var[:, :], ACT.Sqrt, bias=eps[:, 0:1],
                                         scale=1.0 / D).then_inc(std_ready, 1)

            for layer in range(LAYERS):
                if layer:
                    with act.Fori(0, ROUNDS) as i:
                        for s in range(RING):
                            stage(layer, i, s, COUNTED)
                if layer == 0:
                    for slot in range(2):
                        node_batch(0, 0, slot)
                with act.Fori(0 if layer else 1, BATCHES // 2) as i:
                    for slot in range(2):
                        node_batch(layer, i, slot)

        @block.vector
        def _(dve):
            steps = [0]

            def ordered(ins):
                ins.then_inc(dve_step, 1)
                steps[0] += 1
                dve.wait_ge(dve_step, steps[0])

            for handed in handed_back["DVE"]:
                dve.sem_inc(handed, 1)
            nc.vector.memset(src_all[:, LAST:GROUPS, :], 0).then_inc(lists_cleared, 1)
            nc.vector.memset(dst_all[:, LAST:GROUPS, :], NP - 1).then_inc(lists_cleared, 1)
            nc.vector.memset(rows[:, :, :, S - 1:S], 1.0)
            nc.vector.memset(eps[:, :], EPS)
            nc.vector.memset(zeros[:, :], 0.0)
            nc.vector.memset(blank[:, :], 0.0)
            ordered(nc.vector.memset(sums[:, :], 0.0))
            dve.wait_ge(consts_ready, 8)
            nc.vector.tensor_copy(iota, iota_sb[:, :])
            dve.wait_ge(dst_loaded, 3 * DMA)
            ordered(nc.vector.tensor_copy(dst_rel[:, :, :], dst_all))
            nc.vector.tensor_reduce(ends[:, 0, :], dst_rel[:, :, :], axis=X, op=ALU.min)
            nc.vector.tensor_reduce(ends[:, 1, :], dst_rel[:, :, :], axis=X, op=ALU.max).then_inc(ends_ready, 1)

            dve.wait_ge(chunks_loaded, 2 * DMA)
            ordered(nc.vector.tensor_reduce(least[:, :], chunk_dst, axis=X, op=ALU.min))
            ordered(nc.vector.tensor_tensor(chunk_off, chunk_dst,
                                            least[:, :].rearrange("g (c a) -> g c a", a=1).to_broadcast([COUNTED, J, P]),
                                            ALU.subtract))
            ordered(nc.vector.tensor_reduce(reach[:, :], chunk_off.rearrange("g c e -> g (c e)"), axis=X, op=ALU.max))
            nc.vector.tensor_scalar(narrow[:, :], reach[:, :], float(W), None, ALU.is_lt)
            nc.vector.tensor_scalar(wide[:, :], reach[:, :], float(W), None, ALU.is_ge)
            nc.vector.tensor_scalar(chunk_tile, chunk_src, SHIFT, None, ALU.arith_shift_right)
            ordered(nc.vector.tensor_scalar(chunk_low, chunk_src, P - 1, None, ALU.bitwise_and))
            ordered(nc.vector.tensor_scalar(chunk_low_f, chunk_low, 1.0, None, ALU.add))
            ordered(nc.vector.scalar_tensor_tensor(out=chunk_off, in0=chunk_tile, scalar=float(W), in1=chunk_off,
                                                   op0=ALU.mult, op1=ALU.add))
            ordered(nc.vector.tensor_scalar(chunk_key, chunk_off, 1.0, narrow[:, 0:1], ALU.add, ALU.mult))
            nc.vector.tensor_tensor(slot_rows[:, :, :], slot_iota[:, :, :],
                                    least[:, :].rearrange("g (c a) -> g c a", a=1).to_broadcast([COUNTED, J, W]),
                                    ALU.add).then_inc(keys_made, 1)

            dve.wait_ge(ends_turned, 1)
            for e, op in ((0, ALU.min), (1, ALU.max)):
                nc.vector.tensor_reduce(group_ends[:, e, 0:1], deg_ps[:, e * 2 * P:e * 2 * P + P], axis=X, op=op)
                last = nc.vector.tensor_reduce(group_ends[0:GROUPS - P, e, 1:2],
                                               deg_ps[0:GROUPS - P, e * 2 * P + P:(e + 1) * 2 * P], axis=X, op=op)
            ordered(last)
            nc.vector.tensor_copy(masks[:, 0, 0, :], group_ends[:, 0, 0:1].to_broadcast([P, P]))
            nc.vector.tensor_copy(masks[0:GROUPS - P, 1, 0, :], group_ends[0:GROUPS - P, 0, 1:2]
                                  .to_broadcast([GROUPS - P, P])).then_inc(group_ends_ready, 1)
            dve.wait_ge(group_ends_turned, 1)
            ordered(nc.vector.tensor_copy(span[:, :, :],
                                          conv_ps[0:1, 0:2 * GROUPS].rearrange("p (e g) -> p g e", e=2)))
            ordered(nc.vector.tensor_tensor(span[:, :, 1], span[:, :, 1], span[:, :, 0], ALU.subtract))
            ordered(nc.vector.tensor_scalar(span[:, :, 1], span[:, :, 1], SHIFT, None, ALU.arith_shift_right))
            nc.vector.tensor_scalar(span[:, :, 1], span[:, :, 1], 1, None, ALU.add)
            nc.vector.tensor_tensor(dst_rel[:, :, :], dst_rel[:, :, :],
                                    base_ps.rearrange("p (g a) -> p g a", a=1).to_broadcast([P, GROUPS, J]),
                                    ALU.subtract)
            nc.vector.tensor_copy(wide_row[:, :], conv_ps[0:1, BANK:BANK + COUNTED])
            ordered(nc.vector.tensor_reduce(any_wide_f[:, :], conv_ps[0:1, BANK:BANK + COUNTED], axis=X, op=ALU.max))
            nc.vector.tensor_copy(any_wide[:, :], any_wide_f[:, :]).then_inc(group_ends_ready, 1)
            dve.wait_ge(keys_turned, 1)
            ordered(nc.vector.tensor_copy(slot_node[:, :], turn_ps[0:SLOTS, 0:COUNTED]))
            nc.vector.tensor_tensor(slot_node[:, :], slot_node[:, :], base_ps[0:SLOTS, 0:COUNTED], ALU.subtract)
            nc.vector.tensor_copy(keys[:, :, :, :].rearrange("p k c g -> p (k c) g"),
                                  build[:, :, :].rearrange("p b c -> p (b c)")[:, 0:2 * J * 64]
                                  .rearrange("p (k g) -> p k g", g=64)[:, :, 0:COUNTED]).then_inc(lists_ready, 1)
            dve.wait_ge(lists_ready, 1)

            pairs = dve.alloc_register("dve_pairs")
            before = dve.alloc_register("dve_before")
            slot_pairs = dve.alloc_register("dve_slot_pairs")
            dve.reg_mov(pairs, 0)
            dve.reg_mov(slot_pairs, 0)
            span_regs = [dve.alloc_register(f"dve_span{n}") for n in range(2 * RING)]
            slot_span_regs = [dve.alloc_register(f"dve_slot_span{n}") for n in range(2 * PER_ROUND)]

            def take_part(layer, k, node):
                width = D if layer else S
                dve.wait_ge(part_ready, k + 1)
                dve.wait_ge(part_taken, k + 1)
                here = sums[0:width, bass.ds(node, P)]
                return nc.vector.tensor_tensor(here, part[0:width, (k + 1) % 2, 0:P], here, ALU.add)

            def load_spans(regs, g, count):
                dve.load(regs[0:2 * count], span[0:1, bass.ds(g, count), :])

            def mask_pairs(layer, span_of_group, make_mask, between=None):
                node_reg, windows_reg = span_of_group
                windows = dve.snap(windows_reg, min_val=1, max_val=TILES)

                def mask_pair(w):
                    k = dve.snap(pairs, min_val=0, max_val=MAX_PAIRS)
                    make_mask(k, w).then_inc(masks_ready, 1)
                    take_part(layer, k, dve.snap(before, min_val=0, max_val=NP - 1)).then_inc(part_taken, 1)
                    dve.reg_add(before, node_reg, 0)
                    dve.reg_add(node_reg, node_reg, P)
                    dve.reg_add(pairs, pairs, 1)

                mask_pair(0)
                if between:
                    between()
                with dve.If(windows > 1):
                    with dve.Fori(1, windows) as w:
                        mask_pair(w)

            def mask_group(layer, g, span, between=None):
                def make_mask(k, w):
                    return nc.vector.scalar_tensor_tensor(
                        out=masks[:, k % 2, :, :],
                        in0=dst_rel[:, g, :].rearrange("p (j a) -> p j a", a=1).to_broadcast([P, J, P]),
                        scalar=window_base[:, bass.ds(w, 1)],
                        in1=iota.rearrange("p (a n) -> p a n", a=1).to_broadcast([P, J, P]),
                        op0=ALU.subtract, op1=ALU.is_equal)
                mask_pairs(layer, span, make_mask, between)

            def mask_slots(layer, i, s, span):
                g = i * PER_ROUND + s
                dve.wait_ge(slots_summed, i * PER_ROUND + ((layer - 1) * COUNTED + s + 1))
                dve.wait_ge(part_ready, dve.snap(slot_pairs, min_val=0, max_val=MAX_PAIRS) + 1)
                nc.vector.tensor_reduce(slot_sums[:, :], slots_ps.rearrange("p (k d) -> p d k", k=PARTS),
                                        axis=X, op=ALU.add).then_inc(slots_taken, 1)

                def make_mask(k, w):
                    return nc.vector.scalar_tensor_tensor(
                        out=masks[0:SLOTS, k % 2, 0, :],
                        in0=slot_node[:, bass.ds(g, 1)].to_broadcast([SLOTS, P]),
                        scalar=window_base[0:SLOTS, bass.ds(w, 1)],
                        in1=iota[0:SLOTS, :], op0=ALU.subtract, op1=ALU.is_equal)
                mask_pairs(layer, span, make_mask)
                dve.reg_add(slot_pairs, pairs, 0)

            def make_onehots(i, h):
                g = i * BPER_ROUND + h // 2
                half = h % 2
                for c in range(J):
                    n = h * J + c
                    turn = n % 2
                    if not isinstance(i, int) or i or n >= 2:
                        dve.wait_ge(chunk_built, i * (RING * J) + (n - 1))
                    nc.vector.tensor_scalar(is_low[:, turn, :], from_one[:, 0:P], keys[:, 1, c, bass.ds(g, 1)],
                                            None, ALU.is_equal)
                    nc.vector.tensor_scalar(is_key[:, turn, :], from_one[:, half * HALF * W:(half + 1) * HALF * W],
                                            keys[:, 0, c, bass.ds(g, 1)], None,
                                            ALU.is_equal).then_inc(onehots_ready, 1)

            def node_batch(layer, i, slot):
                done = layer * BATCHES
                n = 2 * i + slot
                if layer == 0:
                    dve.wait_ge(deg_ready, n + 1)
                    dve.wait_ge(x_kept, n + 1)
                    nc.vector.tensor_tensor(own[:, slot, :], deg_ps[0:D, 0:B], own[:, slot, :],
                                            ALU.mult).then_inc(own_scaled, 1)
                if layer < LAYERS - 1:
                    dve.wait_ge(act_ready, n + (done + 2))
                    dve.wait_ge(deg_ready, n + (done + 1))
                    nc.vector.tensor_tensor(own[:, slot, :], deg_ps[0:D, 0:B], act_t[:, :],
                                            ALU.mult).then_inc(own_kept, 1)
                    h = node_rows[:, slot, :, :]
                    dve.wait_ge(act_turned, n + (done + 2))
                    if layer or not isinstance(i, int):
                        dve.wait_ge(nodes_stored[slot], (i + layer * BATCHES // 2) * DMA)
                    nc.vector.tensor_copy(h, turned).then_inc(nodes_ready, 1)
                    dve.wait_ge(nodes_ready, n + (done + 2))

                    def ordered_split(ins, step):
                        ins.then_inc(split_step, 1)
                        dve.wait_ge(split_step, n * 4 + (done * 4 + step))

                    to = [parts[:, bass.ds(n * BT, BT), k, :] for k in range(PARTS)]
                    ordered_split(nc.vector.tensor_copy(to[0], h), 1)
                    ordered_split(nc.vector.tensor_tensor(left[:, :, :], h, to[0], ALU.subtract), 2)
                    ordered_split(nc.vector.tensor_copy(to[1], left[:, :, :]), 3)
                    ordered_split(nc.vector.tensor_tensor(to[2], left[:, :, :], to[1], ALU.subtract), 4)
                else:
                    def ordered_norm(ins, step):
                        ins.then_inc(norm_step, 1)
                        dve.wait_ge(norm_step, n * 5 + step)

                    z = node_rows[:, slot, :, :]
                    dve.wait_ge(act_turned, n + (done + 2))
                    dve.wait_ge(x_loaded[slot], (i + (BATCHES // 2 + 1)) * 2 * DMA)
                    dve.wait_ge(nodes_stored[slot], (i * 2 + layer * BATCHES // 2) * DMA)
                    ordered_norm(nc.vector.tensor_tensor(z, turned, x_rows[:, slot, :, :], ALU.add), 1)
                    ordered_norm(nc.vector.tensor_reduce(mean[:, :], z, axis=X, op=ALU.add), 2)
                    ordered_norm(nc.vector.scalar_tensor_tensor(
                        out=z, in0=per_node(mean), scalar=-1.0 / D, in1=z, op0=ALU.mult, op1=ALU.add), 3)
                    ordered_norm(nc.vector.tensor_tensor(left[:, :, :], z, z, ALU.mult), 4)
                    nc.vector.tensor_reduce(var[:, :], left[:, :, :], axis=X, op=ALU.add).then_inc(var_ready, 1)
                    dve.wait_ge(std_ready, n + 1)
                    ordered_norm(nc.vector.reciprocal(rstd[:, :], std[:, :]), 5)
                    nc.vector.tensor_tensor(z, z, per_node(rstd), ALU.mult).then_inc(nodes_ready, 1)

            for layer in range(LAYERS):
                ordered(nc.vector.memset(part[:, :, 0:P], 0.0))
                dve.reg_mov(before, 0)
                if layer:
                    dve.wait_ge(sums_cleared, layer * BATCHES)

                def groups_of_round(i, counted):
                    first_group = COUNTED if layer else 0
                    load_spans(span_regs, i * RING + first_group, RING)
                    if layer and counted:
                        load_spans(slot_span_regs, i * PER_ROUND, PER_ROUND)
                    for s in range(RING):
                        between = (lambda: make_onehots(i, s)) if layer == 0 and s < counted else None
                        mask_group(layer, i * RING + (s + first_group), span_regs[2 * s:2 * s + 2], between)
                        if layer and s < counted:
                            mask_slots(layer, i, s, slot_span_regs[2 * s:2 * s + 2])

                if layer == 0:
                    groups_of_round(0, RING)
                    with dve.Fori(1, BROUNDS) as i:
                        groups_of_round(i, RING)
                    groups_of_round(BROUNDS, 2 * BREST)
                    with dve.Fori(BROUNDS + 1, ROUNDS0) as i:
                        groups_of_round(i, 0)
                else:
                    with dve.Fori(0, CROUNDS) as i:
                        groups_of_round(i, PER_ROUND)
                    with dve.Fori(CROUNDS, ROUNDS) as i:
                        groups_of_round(i, 0)
                if layer:
                    some = dve.value_load(any_wide[0:1, 0:1], min_val=0, max_val=1)
                    with dve.If(some > 0):
                        with dve.Fori(0, COUNTED) as g:
                            is_wide = dve.value_load(wide_row[0:1, bass.ds(g, 1)], min_val=0, max_val=1)
                            with dve.If(is_wide > 0):
                                load_spans(span_regs, g, 1)
                                mask_group(layer, g, span_regs[0:2])
                take_part(layer, dve.snap(pairs, min_val=0, max_val=MAX_PAIRS),
                          dve.snap(before, min_val=0, max_val=NP - 1)).then_inc(layer_summed, 1)
                if layer == 0:
                    for slot in range(2):
                        node_batch(0, 0, slot)
                with dve.Fori(0 if layer else 1, BATCHES // 2) as i:
                    for slot in range(2):
                        node_batch(layer, i, slot)

        @block.tensor
        def _(pe):
            for handed in handed_back["PE"]:
                pe.sem_inc(handed, 1)
            pe.wait_ge(consts_ready, 8)
            pe.wait_ge(ends_ready, 1)
            for e in range(2):
                nc.tensor.transpose(deg_ps[0:P, e * 2 * P:e * 2 * P + P], ends[:, e, 0:P], ident[:, :])
                last = nc.tensor.transpose(deg_ps[0:GROUPS - P, e * 2 * P + P:(e + 1) * 2 * P],
                                           ends[:, e, P:GROUPS], ident[:, :])
            last.then_inc(ends_turned, 1)
            pe.wait_ge(group_ends_ready, 1)
            pe.wait_ge(keys_made, 1)
            nc.tensor.matmul(base_ps[:, 0:P], masks[:, 0, 0, :], ident[:, :], start=True, stop=True)
            nc.tensor.matmul(base_ps[:, P:GROUPS], masks[0:GROUPS - P, 1, 0, :],
                             ident[0:GROUPS - P, 0:GROUPS - P], start=True, stop=True)
            for e in range(2):
                nc.tensor.transpose(conv_ps[0:1, e * GROUPS:e * GROUPS + P], group_ends[:, e, 0:1], ident[:, :])
                nc.tensor.transpose(conv_ps[0:1, e * GROUPS + P:(e + 1) * GROUPS],
                                    group_ends[0:GROUPS - P, e, 1:2], ident[0:GROUPS - P, 0:GROUPS - P])
            nc.tensor.transpose(conv_ps[0:1, BANK:BANK + COUNTED], wide[:, :],
                                ident[0:COUNTED, 0:COUNTED]).then_inc(group_ends_turned, 1)
            pe.wait_ge(group_ends_ready, 2)
            for k, what in enumerate((chunk_key, chunk_low_f)):
                for c in range(J):
                    q, at = divmod((k * J + c) * 64, BANK)
                    nc.tensor.transpose(build[:, q, at:at + COUNTED], what[:, c, :], ident[0:COUNTED, 0:COUNTED])
            nc.tensor.transpose(turn_ps[0:SLOTS, 0:COUNTED], slot_rows[:, :, :].rearrange("g c w -> g (c w)"),
                                ident[0:COUNTED, 0:COUNTED]).then_inc(keys_turned, 1)

            pe.wait_ge(lists_ready, 1)
            pe.wait_ge(w_loaded, 3 * LAYERS * DMA)
            pairs = pe.alloc_register("pe_pairs")
            wides = pe.alloc_register("pe_wides")
            pe.reg_mov(pairs, 0)
            pe.reg_mov(wides, 0)
            span_regs = [pe.alloc_register(f"pe_span{n}") for n in range(2 * RING)]
            slot_span_regs = [pe.alloc_register(f"pe_slot_span{n}") for n in range(2 * PER_ROUND)]

            def load_spans(regs, g, count):
                pe.load(regs[0:2 * count], span[0:1, bass.ds(g, count), :])

            def mark(layer):
                spare = build[0:1, 3, BANK - 1:BANK] if layer else turn_ps[0:1, BANK - 1:BANK]
                return nc.tensor.matmul(spare, blank[:, :], blank[:, :], start=True, stop=True)

            def sum_pair(width, operands, between=None):
                k = pe.snap(pairs, min_val=0, max_val=MAX_PAIRS)
                pe.wait_ge(masks_ready, k + 1)
                pe.wait_ge(part_taken, k + 1)
                products = operands(k % 2)
                for j, (values, rhs) in enumerate(products):
                    mm = nc.tensor.matmul(part[0:width, k % 2, 0:P], values, rhs,
                                          start=(j == 0), stop=(j == len(products) - 1))
                    if j == len(products) - 1:
                        mm.then_inc(part_ready, 1)
                    if between:
                        between(j)
                pe.reg_add(pairs, pairs, 1)

            def sum_pairs(windows_reg, width, operands, between=None):
                windows = pe.snap(windows_reg, min_val=1, max_val=TILES)
                sum_pair(width, operands, between)
                with pe.If(windows > 1):
                    with pe.Fori(1, windows):
                        sum_pair(width, operands)

            def sum_rows(layer, windows_reg, s, between=None):
                width = D if layer else S
                sum_pairs(windows_reg, width, lambda turn: [(rows[:, s, j, 0:width], masks[:, turn, j, :]) for j in range(J)],
                          between)

            def sum_slots(windows_reg):
                sum_pairs(windows_reg, D, lambda turn: [(slot_sums[:, :], masks[0:SLOTS, turn, 0, :])])

            def build_counts(i, h):
                def build_chunk(c):
                    n = h * J + c
                    turn = n % 2
                    pe.wait_ge(onehots_ready, i * (RING * J) + (n + 1))
                    if not isinstance(i, int) or i or n >= 2:
                        pe.wait_ge(chunk_kept, i * (RING * J) + (n - 1))
                    for q in range(2):
                        last = nc.tensor.matmul(build[:, 2 * turn + q, 0:QUARTER], is_low[:, turn, :],
                                                is_key[:, turn, q * QUARTER:(q + 1) * QUARTER],
                                                start=True, stop=True)
                    last.then_inc(chunk_built, 1)
                return build_chunk

            def apply_counts(layer, i, s):
                pe.wait_ge(slots_taken, i * PER_ROUND + ((layer - 1) * COUNTED + s + 1))
                for half, tiles in enumerate(HALVES):
                    h = 2 * s + half
                    r = h % CRING
                    use = i * 2 + ((layer - 1) * CROUNDS * 2 + h // CRING)
                    pe.wait_ge(block_loaded[r], (use + 1) * DMA)
                    for t in tiles:
                        last = nc.tensor.matmul(slots_ps, blocks[:, r, t - half * HALF, :],
                                                parts[:, t, :, :].rearrange("p k d -> p (k d)"),
                                                start=(t == 0), stop=(t == TILES - 1))
                    if half == 0:
                        last.then_inc(block_used[r], 1)
                last.then_inc(slots_summed, 1)
                mark(layer).then_inc(block_used[r], 1)

            def groups_of_round(layer, i, counted):
                load_spans(span_regs, i * RING + (COUNTED if layer else 0), RING)
                if layer and counted:
                    load_spans(slot_span_regs, i * PER_ROUND, PER_ROUND)
                uses = pe.compute_val(i + (USES[layer] + 1))
                landed = pe.compute_val(uses * (J * DMA))
                for s in range(RING):
                    if layer and s < counted:
                        apply_counts(layer, i, s)
                    pe.wait_ge(lists_ready, 1)
                    pe.wait_ge(rows_landed[s], landed)
                    if layer == 0:
                        pe.wait_ge(attr_copied[s], uses)
                    between = build_counts(i, s) if layer == 0 and s < counted else None
                    sum_rows(layer, span_regs[2 * s + 1], s, between)
                    mark(layer).then_inc(rows_used[s], 1)
                    if layer and s < counted:
                        sum_slots(slot_span_regs[2 * s + 1])

            for layer in range(LAYERS):
                if layer == 0:
                    groups_of_round(0, 0, RING)
                    with pe.Fori(1, BROUNDS) as i:
                        groups_of_round(0, i, RING)
                    groups_of_round(0, BROUNDS, 2 * BREST)
                    with pe.Fori(BROUNDS + 1, ROUNDS0) as i:
                        groups_of_round(0, i, 0)
                else:
                    pe.wait_ge(split_step, layer * BATCHES * 4)
                    with pe.Fori(0, CROUNDS) as i:
                        groups_of_round(layer, i, PER_ROUND)
                    with pe.Fori(CROUNDS, ROUNDS) as i:
                        groups_of_round(layer, i, 0)
                if layer:
                    some = pe.value_load(any_wide[0:1, 0:1], min_val=0, max_val=1)
                    with pe.If(some > 0):
                        with pe.Fori(0, COUNTED) as g:
                            is_wide = pe.value_load(wide_row[0:1, bass.ds(g, 1)], min_val=0, max_val=1)
                            with pe.If(is_wide > 0):
                                landed = pe.compute_val((pe.snap(wides, min_val=0, max_val=LAYERS * COUNTED) + 1) * (J * DMA))
                                pe.wait_ge(lists_ready, 1)
                                pe.wait_ge(wide_landed, landed)
                                load_spans(span_regs, g, 1)
                                sum_rows(layer, span_regs[1], 0)
                                mark(layer).then_inc(wide_used, 1)
                                pe.reg_add(wides, wides, 1)

                done = layer * BATCHES
                pe.wait_ge(layer_summed, layer + 1)
                with pe.Fori(0, BATCHES // 2) as i:
                    for slot in range(2):
                        b = pe.compute_val(2 * i + slot)
                        handed = pe.compute_val(b + (done + 1))
                        made = pe.compute_val(b + (done + 2))
                        loaded = pe.compute_val((i + 1) * (2 * DMA))
                        scaled = pe.compute_val(b + 1)
                        owned = pe.compute_val((i + ((layer - 1) * BATCHES // 2 + 1)) * DMA) if layer else None
                        if layer < LAYERS - 1:
                            pe.wait_ge(own_kept, handed)
                            for lo, hi in CUTS:
                                last = nc.tensor.matmul(deg_ps[0:D, lo:hi], pick_deg[:, :],
                                                        sums[:, bass.ds(b * B + lo, hi - lo)], start=True, stop=True)
                            last.then_inc(deg_ready, 1)
                        if layer == 0:
                            pe.wait_ge(consts_ready, 8)
                            pe.wait_ge(x_loaded[slot], loaded)
                            for t in range(BT):
                                last = nc.tensor.transpose(x_ps[0:D, t * P:(t + 1) * P], x_rows[:, slot, t, :],
                                                           ident[:, :])
                            last.then_inc(x_turned, 1)
                            pe.wait_ge(w_loaded, 3 * LAYERS * DMA)
                            pe.wait_ge(own_scaled, scaled)
                        else:
                            pe.wait_ge(w_loaded, 3 * LAYERS * DMA)
                            pe.wait_ge(own_loaded[slot], owned)
                        pe.wait_ge(act_ready, handed)
                        for lo, hi in CUTS:
                            nc.tensor.matmul(conv_ps[0:D, lo:hi], w_own[layer][:, :], own[:, slot, lo:hi],
                                             start=True, stop=False)
                            last = nc.tensor.matmul(conv_ps[0:D, lo:hi], w_sum[layer][:, :],
                                                    sums[:, bass.ds(b * B + lo, hi - lo)], start=False, stop=True)
                        last.then_inc(conv_ready, 1)
                        pe.wait_ge(consts_ready, 8)
                        pe.wait_ge(act_ready, made)
                        pe.wait_ge(nodes_ready, handed)
                        for t in range(BT):
                            last = nc.tensor.transpose(turn_ps[:, t * D:(t + 1) * D], act_t[:, t * P:(t + 1) * P],
                                                       ident[0:D, 0:D])
                        last.then_inc(act_turned, 1)


_INS = ["x", "src", "dst", "edge_attr_16", "L0_gnn_W1", "L0_gnn_b1", "L0_gnn_W2", "L0_gnn_b2",
        "L0_gnn_W3", "L0_gnn_b3"]


def kernel(**inputs):
    import numpy as _np
    import concourse.bacc as _bacc
    from concourse import mybir as _mybir
    from concourse.bass_utils import run_bass_kernel_spmd as _run

    nc = _bacc.Bacc("TRN2", target_bir_lowering=False, num_devices=1)
    arrays, aps = {}, {}
    for name in _INS:
        a = _np.ascontiguousarray(inputs[name])
        arrays[f"in_{name}"] = a
        aps[name] = nc.dram_tensor(f"in_{name}", a.shape, _mybir.dt.from_np(a.dtype), kind="ExternalInput").ap()
    out = nc.dram_tensor("out_0", inputs["x"].shape, _mybir.dt.float32, kind="ExternalOutput").ap()
    weights = [(aps[f"L0_gnn_W{n}"], aps[f"L0_gnn_b{n}"]) for n in (1, 2, 3)]
    gnn_kernel(nc, aps["x"], aps["src"], aps["dst"], aps["edge_attr_16"], weights, out)
    r = _run(nc, [arrays], core_ids=[0])
    return r.results[0]["out_0"]
```

```python
import concourse.bass as bass
from concourse import mybir
from contextlib import ExitStack


def gnn_kernel(nc, x, src, dst, edge_attr, weights, out):
    fp32 = mybir.dt.float32
    bf16 = mybir.dt.bfloat16
    fp16 = mybir.dt.float16
    i32 = mybir.dt.int32
    ALU = mybir.AluOpType
    ACT = mybir.ActivationFunctionType
    X = mybir.AxisListType.X

    N, D = x.shape
    E, ED = edge_attr.shape
    P = nc.NUM_PARTITIONS
    LAYERS = len(weights)
    TILES = -(-N // P)
    NP = TILES * P
    NODE_REST = N - (TILES - 1) * P
    J = 11
    W = 11
    SLOTS = J * W
    GROUP = P * J
    RING = 4
    ALL_GROUPS = -(-E // GROUP)
    ROUNDS0 = -(-ALL_GROUPS // RING)
    GROUPS = ROUNDS0 * RING
    COUNTED = 75
    PER_ROUND = RING
    CROUNDS, CREST = divmod(COUNTED, PER_ROUND)
    ROUNDS = (ALL_GROUPS - COUNTED) // RING
    assert COUNTED + ROUNDS * RING == ALL_GROUPS and CREST and CROUNDS < ROUNDS
    assert ALL_GROUPS > P >= GROUPS - P
    LAST = ALL_GROUPS - 1
    REST = E - LAST * GROUP
    REST_P, REST_J = divmod(REST, J)
    S = D + ED + 1
    PARTS = 3
    THIRD = 34
    THIRDS = [range(0, THIRD), range(THIRD, 2 * THIRD), range(2 * THIRD, TILES)]
    BPER_ROUND = RING // 2
    BROUNDS, BREST = divmod(COUNTED, BPER_ROUND)
    assert BREST == 1 and BROUNDS < ROUNDS0
    PEELED = min(BROUNDS, ROUNDS0 - 2)
    BANK = 512
    KEYS = THIRD * W
    CRING = 4
    PLACED = [len(range(r, COUNTED * len(THIRDS), CRING)) for r in range(CRING)]
    BT = 7
    B = BT * P
    BATCHES = TILES // BT
    assert BATCHES * BT == TILES and KEYS <= BANK and SLOTS <= P
    KEYS_IN_BANK = BANK // COUNTED
    SHIFT = P.bit_length() - 1
    EPS = 1e-5
    CONSTS = 6 + 2 * LAYERS
    STEPS = 6
    DMA = 16
    USES = [0] + [ROUNDS0 + ROUNDS * n for n in range(LAYERS)]
    MAX_PAIRS = LAYERS * 2 * GROUPS * TILES

    feats = [x] + [nc.dram_tensor(f"feats_{n}", (NP, D), fp32).ap() for n in range(1, LAYERS)]
    counts = nc.dram_tensor("counts", (COUNTED, len(THIRDS), P, THIRD * SLOTS), bf16).ap()
    src_groups = src[0:LAST * GROUP].rearrange("(g p j) -> p g j", p=P, j=J)
    dst_groups = dst[0:LAST * GROUP].rearrange("(g p j) -> p g j", p=P, j=J)
    attr_groups = edge_attr[0:LAST * GROUP, :].rearrange("(g p j) c -> g p (j c)", p=P, j=J)

    ctx = ExitStack()
    with ctx:
        def sb(name, shape, dt=fp32):
            return ctx.enter_context(nc.sbuf_tensor(name, shape, dt))

        def pb(name, shape):
            return ctx.enter_context(nc.psum_tensor(name, shape, fp32))

        def sem(name):
            return ctx.enter_context(nc.semaphore(name))

        sums = sb("sums", [S, NP + P])
        rows = sb("rows", [P, RING, J, S])
        masks = sb("masks", [P, 2, J, P])
        src_all = sb("src_all", [P, GROUPS, J], i32)
        dst_rel = sb("dst_rel", [P, GROUPS, J])
        src_stage = sb("src_stage", [P, RING, J], i32)
        attr_stage = sb("attr_stage", [P, RING, J * ED])
        ident = sb("ident", [P, P])
        iota_sb = sb("iota_sb", [P, P])
        from_one = sb("from_one", [P, 3 * KEYS], fp16)
        window_base = sb("window_base", [P, TILES])
        ends = sb("ends", [P, 2, GROUPS])
        group_ends = sb("group_ends", [P, 2, 2])
        span = sb("span", [1, GROUPS, 2], i32)
        w_own = [sb(f"w_own{n}", [D, D]) for n in range(LAYERS)]
        w_sum = [sb(f"w_sum{n}", [S, D + 1]) for n in range(LAYERS)]

        parts = sb("parts", [P, TILES, PARTS, D], bf16)
        blocks_flat = sb("blocks", [P, CRING * THIRD * SLOTS], bf16)
        blocks = blocks_flat[:, :].rearrange("p (r t s) -> p r t s", r=CRING, t=THIRD)
        is_low = sb("is_low", [P, 2, P], bf16)
        is_key = sb("is_key", [P, 2, 2 * KEYS], bf16)
        keys = sb("keys", [P, 2, J, COUNTED])
        least = sb("least", [COUNTED, J])
        reach = sb("reach", [COUNTED, 1])
        narrow = sb("narrow", [COUNTED, 1])
        wide = sb("wide", [COUNTED, 1])
        slot_iota = sb("slot_iota", [COUNTED, J, W])
        slot_rows = sb("slot_rows", [COUNTED, J, W])
        slot_node = sb("slot_node", [SLOTS, COUNTED])
        wide_row = sb("wide_row", [1, COUNTED], i32)
        any_wide_f = sb("any_wide_f", [1, 1])
        any_wide = sb("any_wide", [1, 1], i32)
        slot_sums = sb("slot_sums", [SLOTS, D])

        h_rows = sb("h_rows", [P, 2, BT, D])
        h_turned = sb("h_turned", [D, 2, B])
        batch_sums = sb("batch_sums", [S, 2, B])
        z = sb("z", [P, BT, D])
        node_rows = sb("node_rows", [P, 2, BT, D])
        x_rows = sb("x_rows", [P, 2, BT, D])
        left = sb("left", [P, BT, D])
        deg = sb("deg", [P, BT])
        mean = sb("mean", [P, BT])
        var = sb("var", [P, BT])
        std = sb("std", [P, BT])
        rstd = sb("rstd", [P, BT])
        eps = sb("eps", [P, 1])
        zeros = sb("zeros", [D, 1])
        blank = sb("blank", [P, 1], bf16)

        early = blocks_flat[:, :].bitcast(i32)
        dst_all = early[:, 0:GROUPS * J].rearrange("p (g j) -> p g j", j=J)
        early = parts[0:COUNTED, :, :, :].rearrange("p t k d -> p (t k d)").bitcast(i32)

        def early_list(n):
            return early[:, n * GROUP:(n + 1) * GROUP].rearrange("g (c e) -> g c e", c=J)

        chunk_dst, chunk_src, chunk_tile, chunk_low = (early_list(n) for n in range(4))
        chunk_off, chunk_key = (early_list(n).bitcast(fp32) for n in range(4, 6))
        chunk_low_f = chunk_dst.bitcast(fp32)

        part = pb("part", [P, 2, BANK])
        build = pb("build", [P, 4, BANK])
        turn_ps = pb("turn_ps", [P, BANK])
        iota_ps = pb("iota_ps", [P, BANK])
        iota = iota_ps[:, 0:P]
        base_ps = turn_ps[:, P:P + GROUPS]
        ends_ps = build[:, 0:2, :].rearrange("p b c -> p (b c)")
        lists_ps = build[:, 2:4, :].rearrange("p b c -> p (b c)")
        turn_h_ps = part[:, :, :].rearrange("p b c -> p (b c)")
        own_ps = [build[:, n, 0:BT * D].rearrange("p (t d) -> p t d", d=D) for n in range(2)]
        rest_ps = [build[:, 2 + n, 0:BT * (D + 1)].rearrange("p (t d) -> p t d", d=D + 1) for n in range(2)]
        slots_ps = turn_ps[0:SLOTS, 0:PARTS * D]

        def per_node(v):
            return v[:, :].rearrange("p (t a) -> p t a", a=1).to_broadcast([P, BT, D])

        consts_ready = sem("consts_ready")
        lists_cleared = sem("lists_cleared")
        src_loaded = sem("src_loaded")
        dst_loaded = sem("dst_loaded")
        chunks_loaded = sem("chunks_loaded")
        w_loaded = sem("w_loaded")
        ends_ready = sem("ends_ready")
        ends_turned = sem("ends_turned")
        group_ends_ready = sem("group_ends_ready")
        group_ends_turned = sem("group_ends_turned")
        keys_made = sem("keys_made")
        keys_turned = sem("keys_turned")
        lists_ready = sem("lists_ready")
        src_staged = [sem(f"src_staged{s}") for s in range(RING)]
        rows_landed = [sem(f"rows_landed{s}") for s in range(RING)]
        rows_used = [sem(f"rows_used{s}") for s in range(RING)]
        attr_landed = [sem(f"attr_landed{s}") for s in range(RING)]
        attr_copied = [sem(f"attr_copied{s}") for s in range(RING)]
        masks_ready = sem("masks_ready")
        part_ready = sem("part_ready")
        part_taken = sem("part_taken")
        onehots_ready = sem("onehots_ready")
        chunk_built = sem("chunk_built")
        chunk_kept = sem("chunk_kept")
        two_thirds_stored = sem("two_thirds_stored")
        third_stored = [sem(f"third_stored{b}") for b in range(BPER_ROUND)]
        block_loaded = [sem(f"block_loaded{r}") for r in range(CRING)]
        block_used = [sem(f"block_used{r}") for r in range(CRING)]
        slots_summed = sem("slots_summed")
        slots_taken = sem("slots_taken")
        wide_staged = sem("wide_staged")
        wide_landed = sem("wide_landed")
        wide_used = sem("wide_used")
        layer_summed = sem("layer_summed")
        h_loaded = [sem(f"h_loaded{b}") for b in range(2)]
        x_loaded = [sem(f"x_loaded{b}") for b in range(2)]
        h_in_psum = sem("h_in_psum")
        h_kept = sem("h_kept")
        sums_kept = sem("sums_kept")
        conv_ready = sem("conv_ready")
        conv_taken = sem("conv_taken")
        sums_cleared = sem("sums_cleared")
        nodes_ready = sem("nodes_ready")
        nodes_stored = [sem(f"nodes_stored{b}") for b in range(2)]
        dve_step = sem("dve_step")
        node_step = sem("node_step")
        square_ready = sem("square_ready")
        var_ready = sem("var_ready")
        std_ready = sem("std_ready")

        handed_back = {"PE": [(made, 1) for made in (*rows_used, *block_used, part_ready, wide_used)]
                       + [(conv_ready, 2)],
                       "DVE": [(part_taken, 1), (slots_taken, 1), (conv_taken, 2)],
                       "ACT": [(nodes_ready, 1)]}

        def slots_building(i):
            return RING if i < BROUNDS else 2 * BREST if i == BROUNDS else 0

        def placed_before(layer, i, u):
            return i * (len(THIRDS) * PER_ROUND // CRING) + ((layer - 1) * PLACED[u % CRING] + u // CRING)

        block = ctx.enter_context(nc.Block())

        @block.sync
        def _(sp):
            sp.wait_ge(lists_cleared, 2)
            for edges, groups, held, loaded in ((src, src_groups, src_all, src_loaded),
                                                (dst, dst_groups, dst_all, dst_loaded)):
                sp.dma_start(held[:, 0:LAST, :], groups).then_inc(loaded, DMA)
                tail = edges[LAST * GROUP:LAST * GROUP + REST_P * J].rearrange("(p j) -> p j", j=J)
                sp.dma_start(held[0:REST_P, LAST, :], tail).then_inc(loaded, DMA)
                tail = edges[E - REST_J:E].rearrange("(p j) -> p j", p=1)
                sp.dma_start(held[REST_P:REST_P + 1, LAST, 0:REST_J], tail).then_inc(loaded, DMA)
            for edges, held in ((dst, chunk_dst), (src, chunk_src)):
                sp.dma_start(held, edges[0:COUNTED * GROUP].rearrange("(g c e) -> g c e", c=J, e=P)
                             ).then_inc(chunks_loaded, DMA)

            def load_attr(i, s):
                g = i * RING + s
                if not isinstance(i, int) or g < LAST:
                    sp.dma_start(attr_stage[:, s, :], attr_groups[g, :, :]).then_inc(attr_landed[s], DMA)
                elif g == LAST:
                    sp.dma_start(attr_stage[0:REST_P, s, :],
                                 edge_attr[LAST * GROUP:LAST * GROUP + REST_P * J, :]
                                 .rearrange("(p j) c -> p (j c)", j=J)).then_inc(attr_landed[s], DMA)
                    sp.dma_start(attr_stage[REST_P:REST_P + 1, s, 0:REST_J * ED],
                                 edge_attr[E - REST_J:E, :].rearrange("(p j) c -> p (j c)", p=1)
                                 ).then_inc(attr_landed[s], DMA)

            for s in range(RING):
                load_attr(0, s)
            for n, (w, b) in enumerate(weights):
                sp.dma_start(w_own[n][:, :], w[0:D, :]).then_inc(w_loaded, DMA)
                sp.dma_start(w_sum[n][0:D + ED, 0:D], w[D:2 * D + ED, :]).then_inc(w_loaded, DMA)
                sp.dma_start(w_sum[n][D + ED:S, 0:D], b.rearrange("(a d) -> a d", a=1)).then_inc(w_loaded, DMA)

            def store_counts(i, s):
                b = s // 2
                sp.wait_ge(chunk_kept, (i * RING + (s + 1)) * J)
                if s % 2 == 0:
                    sp.dma_start(counts[i * BPER_ROUND + b, 0:2, :, :].rearrange("u p c -> p u c"),
                                 blocks[:, 0:2, :, :].rearrange("p u t s -> p u (t s)")
                                 ).then_inc(two_thirds_stored, DMA)
                else:
                    sp.dma_start(counts[i * BPER_ROUND + b, 2, :, :],
                                 blocks[:, 2 + b, :, :].rearrange("p t s -> p (t s)")
                                 ).then_inc(third_stored[b], DMA)

            def first_round(i, building, more=True):
                for s in range(RING):
                    if more:
                        sp.wait_ge(attr_copied[s], i + 1)
                        load_attr(i + 1, s)
                    if s < building:
                        store_counts(i, s)

            with sp.Fori(0, PEELED) as i:
                first_round(i, RING)
            for i in range(PEELED, ROUNDS0):
                first_round(i, slots_building(i), i < ROUNDS0 - 1)

            def load_rows(table, into, loaded, batch, slot):
                last = isinstance(batch, int) and batch == BATCHES - 1
                count = NODE_REST if last and table is x else P
                sp.dma_start(into[:, slot, 0:BT - 1, :],
                             table[bass.ds(batch * B, (BT - 1) * P), :].rearrange("(t p) d -> p t d", p=P)
                             ).then_inc(loaded[slot], DMA)
                sp.dma_start(into[0:count, slot, BT - 1, :],
                             table[bass.ds(batch * B + (BT - 1) * P, count), :]).then_inc(loaded[slot], DMA)

            def store_out(batch, slot):
                last = isinstance(batch, int) and batch == BATCHES - 1
                count = NODE_REST if last else P
                sp.dma_start(out[bass.ds(batch * B, (BT - 1) * P), :].rearrange("(t p) d -> p t d", p=P),
                             node_rows[:, slot, 0:BT - 1, :]).then_inc(nodes_stored[slot], DMA)
                sp.dma_start(out[bass.ds(batch * B + (BT - 1) * P, count), :],
                             node_rows[0:count, slot, BT - 1, :]).then_inc(nodes_stored[slot], DMA)

            def node_batch(layer, i, slot, ahead):
                batch = 2 * i + slot
                done = layer * BATCHES
                if ahead:
                    sp.wait_ge(h_in_psum, 2 * i + (done + slot + 1))
                    load_rows(feats[layer], h_rows, h_loaded, batch + 2, slot)
                sp.wait_ge(nodes_ready, 2 * i + (done + slot + 2))
                if layer < LAYERS - 1:
                    table = feats[layer + 1].rearrange("(b t p) d -> b p t d", p=P, t=BT)
                    sp.dma_start(table[batch, :, :, :], node_rows[:, slot, :, :]).then_inc(nodes_stored[slot], DMA)
                else:
                    store_out(batch, slot)
                    if ahead:
                        load_rows(x, x_rows, x_loaded, batch + 2, slot)

            for layer in range(LAYERS):
                if layer:
                    if layer == 1:
                        sp.wait_ge(two_thirds_stored, COUNTED * DMA)
                        for b in range(BPER_ROUND):
                            sp.wait_ge(third_stored[b], len(range(b, COUNTED, BPER_ROUND)) * DMA)
                    for slot in range(2):
                        sp.wait_ge(nodes_stored[slot], layer * BATCHES // 2 * DMA)
                        load_rows(feats[layer], h_rows, h_loaded, slot, slot)

                    def load_blocks(i, count):
                        for u in range(len(THIRDS) * count):
                            r = u % CRING
                            sp.wait_ge(block_used[r], placed_before(layer, i, u) + 1)
                            sp.dma_start(blocks[:, r, :, :].rearrange("p t s -> p (t s)"),
                                         counts[i * PER_ROUND + u // len(THIRDS), u % len(THIRDS), :, :]
                                         ).then_inc(block_loaded[r], DMA)

                    with sp.Fori(0, CROUNDS) as i:
                        load_blocks(i, PER_ROUND)
                    load_blocks(CROUNDS, CREST)
                for slot in range(2):
                    if layer == 0:
                        load_rows(x, h_rows, h_loaded, slot, slot)
                    if layer == LAYERS - 1:
                        load_rows(x, x_rows, x_loaded, slot, slot)
                with sp.Fori(0, BATCHES // 2 - 2) as i:
                    for slot in range(2):
                        node_batch(layer, i, slot, True)
                for i in range(BATCHES // 2 - 2, BATCHES // 2):
                    for slot in range(2):
                        node_batch(layer, i, slot, i < BATCHES // 2 - 1)
            for slot in range(2):
                sp.wait_ge(nodes_stored[slot], DMA * (LAYERS + 1) * BATCHES // 2)

        @block.gpsimd
        def _(pool):
            nc.gpsimd.iota(iota_sb[:, :], pattern=[[1, P]], base=0, channel_multiplier=0,
                           allow_small_or_imprecise_dtypes=True).then_inc(consts_ready, 1)
            nc.gpsimd.iota(window_base[:, :], pattern=[[P, TILES]], base=0, channel_multiplier=0,
                           allow_small_or_imprecise_dtypes=True).then_inc(consts_ready, 1)
            nc.gpsimd.iota(from_one[:, :], pattern=[[1, 3 * KEYS]], base=1, channel_multiplier=0,
                           allow_small_or_imprecise_dtypes=True).then_inc(consts_ready, 1)
            nc.gpsimd.iota(slot_iota[:, :, :], pattern=[[0, J], [1, W]], base=0, channel_multiplier=0,
                           allow_small_or_imprecise_dtypes=True).then_inc(consts_ready, 1)
            nc.gpsimd.memset(ident[:, :], 0.0).then_inc(consts_ready, 1)
            for w in w_sum:
                nc.gpsimd.memset(w[:, D:D + 1], 0.0).then_inc(consts_ready, 1)
            pool.wait_ge(consts_ready, 5 + LAYERS)
            nc.gpsimd.affine_select(out=ident[:, :], in_=ident[:, :], compare_op=ALU.not_equal, fill=1.0,
                                    base=0, pattern=[[-1, P]], channel_multiplier=1).then_inc(consts_ready, 1)
            for w in w_sum:
                nc.gpsimd.affine_select(out=w[:, D:D + 1], in_=w[:, D:D + 1], compare_op=ALU.not_equal, fill=1.0,
                                        base=-(S - 1), pattern=[[0, 1]], channel_multiplier=1
                                        ).then_inc(consts_ready, 1)

            def gather(layer, s, landed):
                for j in range(J):
                    nc.gpsimd.indirect_dma_start(
                        rows[:, s, j, 0:D], None, feats[layer],
                        bass.IndirectOffsetOnAxis(ap=src_stage[:, s, j:j + 1], axis=0),
                    ).then_inc(landed, DMA)

            wides = pool.alloc_register("pool_wides")
            pool.reg_mov(wides, 0)
            for layer in range(LAYERS):
                if layer:
                    for slot in range(2):
                        pool.wait_ge(nodes_stored[slot], DMA * layer * BATCHES // 2)
                with pool.Fori(0, ROUNDS if layer else ROUNDS0) as i:
                    use = pool.compute_val(i + (USES[layer] + 1))
                    for s in range(RING):
                        pool.wait_ge(src_loaded, 3 * DMA)
                        pool.wait_ge(src_staged[s], use)
                        pool.wait_ge(rows_used[s], use)
                        gather(layer, s, rows_landed[s])
                if layer:
                    pool.wait_ge(lists_ready, 1)
                    pool.wait_ge(rows_used[0], USES[layer + 1] + 1)
                    some = pool.value_load(any_wide[0:1, 0:1], min_val=0, max_val=1)
                    with pool.If(some > 0):
                        with pool.Fori(0, COUNTED) as g:
                            is_wide = pool.value_load(wide_row[0:1, bass.ds(g, 1)], min_val=0, max_val=1)
                            with pool.If(is_wide > 0):
                                count = pool.snap(wides, min_val=0, max_val=LAYERS * COUNTED)
                                use = pool.compute_val(count + 1)
                                pool.wait_ge(wide_used, use)
                                nc.gpsimd.tensor_copy(src_stage[:, 0, :], src_all[:, g, :]).then_inc(wide_staged, 1)
                                pool.wait_ge(src_loaded, 3 * DMA)
                                pool.wait_ge(wide_staged, use)
                                gather(layer, 0, wide_landed)
                                pool.reg_add(wides, wides, 1)
                if layer < LAYERS - 1:
                    with pool.Fori(0, BATCHES) as b:
                        kept = pool.compute_val(b + (layer * BATCHES + 1))
                        pool.wait_ge(consts_ready, CONSTS)
                        pool.wait_ge(sums_kept, kept)
                        nc.gpsimd.tensor_copy(sums[0:D, bass.ds(b * B, B)],
                                              zeros[:, :].to_broadcast([D, B])).then_inc(sums_cleared, 1)

        @block.scalar
        def _(act):
            for handed, count in handed_back["ACT"]:
                act.sem_inc(handed, count)

            def stage(layer, i, s, first_group):
                if layer or not isinstance(i, int) or i:
                    act.wait_ge(rows_landed[s], (i + USES[layer]) * (J * DMA))
                nc.scalar.copy(src_stage[:, s, :], src_all[:, i * RING + (first_group + s), :]).then_inc(src_staged[s], 1)

            def place_attr(i, s):
                g = i * RING + s
                static = isinstance(i, int)
                loads = i + 1 if not static or g < LAST else i + 2 if g == LAST else i
                act.wait_ge(attr_landed[s], loads * DMA)
                act.wait_ge(rows_used[s], i + 1)
                nc.scalar.copy(rows[:, s, :, D:D + ED],
                               attr_stage[:, s, :].rearrange("p (j c) -> p j c", c=ED)
                               ).then_inc(attr_copied[s], 1)

            def keep_counts(i, s):
                uses = i * BPER_ROUND + s // 2 if s % 2 == 0 else i
                if not isinstance(i, int) or uses:
                    act.wait_ge(two_thirds_stored if s % 2 == 0 else third_stored[s // 2], uses * DMA)
                for c in range(J):
                    act.wait_ge(chunk_built, i * (RING * J) + (s * J + c + 1))
                    bank = (s * J + c) % 2 * 2
                    if s % 2 == 0:
                        nc.scalar.copy(
                            blocks[:, 0:2, :, c * W:(c + 1) * W],
                            build[:, bank:bank + 2, 0:KEYS].rearrange("p b (t w) -> p b t w", w=W),
                        ).then_inc(chunk_kept, 1)
                    else:
                        nc.scalar.copy(
                            blocks[:, 2 + s // 2, :, c * W:(c + 1) * W],
                            build[:, bank, 0:KEYS].rearrange("p (t w) -> p t w", w=W),
                        ).then_inc(chunk_kept, 1)

            def first_round(i, building, more=True):
                for s in range(RING):
                    if s == 0:
                        stage(0, i, RING - 1, 0)
                    elif more:
                        stage(0, i + 1, s - 1, 0)
                    if s < RING - 1:
                        place_attr(i, s + 1)
                    elif more:
                        place_attr(i + 1, 0)
                    if s < building:
                        keep_counts(i, s)

            act.wait_ge(src_loaded, 3 * DMA)
            for s in range(RING - 1):
                stage(0, 0, s, 0)
            place_attr(0, 0)
            first_round(0, RING)
            with act.Fori(1, PEELED) as i:
                first_round(i, RING)
            for i in range(PEELED, ROUNDS0):
                first_round(i, slots_building(i), i < ROUNDS0 - 1)

            def keep_h(layer, b, slot):
                act.wait_ge(h_in_psum, b + (layer * BATCHES + 1))
                act.wait_ge(conv_ready, b + (layer * BATCHES + 1))
                nc.scalar.copy(batch_sums[:, slot, :], sums[:, bass.ds(b * B, B)]).then_inc(sums_kept, 1)
                nc.scalar.copy(h_turned[:, slot, :], turn_h_ps[0:D, 0:B]).then_inc(h_kept, 1)

            def node_batch(layer, i, slot):
                b = 2 * i + slot
                if not isinstance(i, int) or b + 1 < BATCHES:
                    keep_h(layer, b + 1, 1 - slot)
                if layer < LAYERS - 1:
                    act.wait_ge(conv_taken, b + (layer * BATCHES + 3))
                    if layer or not isinstance(i, int) or i:
                        act.wait_ge(nodes_stored[slot], (i + layer * BATCHES // 2) * DMA)
                    nc.scalar.activation(node_rows[:, slot, :, :], z[:, :, :], ACT.Relu).then_inc(nodes_ready, 1)
                else:
                    act.wait_ge(var_ready, b + 1)
                    nc.scalar.activation(std[:, :], var[:, :], ACT.Sqrt, bias=eps[:, 0:1],
                                         scale=1.0 / D).then_inc(std_ready, 1)

            for layer in range(LAYERS):
                if layer:
                    with act.Fori(0, ROUNDS) as i:
                        for s in range(RING):
                            stage(layer, i, s, COUNTED)
                keep_h(layer, 0, 0)
                if layer == 0:
                    for slot in range(2):
                        node_batch(0, 0, slot)
                with act.Fori(0 if layer else 1, BATCHES // 2 - 1) as i:
                    for slot in range(2):
                        node_batch(layer, i, slot)
                for slot in range(2):
                    node_batch(layer, BATCHES // 2 - 1, slot)

        @block.vector
        def _(dve):
            steps = [0]

            def ordered(ins):
                ins.then_inc(dve_step, 1)
                steps[0] += 1
                dve.wait_ge(dve_step, steps[0])

            for handed, count in handed_back["DVE"]:
                dve.sem_inc(handed, count)
            nc.vector.memset(src_all[:, LAST:GROUPS, :], 0).then_inc(lists_cleared, 1)
            nc.vector.memset(dst_all[:, LAST:GROUPS, :], NP - 1).then_inc(lists_cleared, 1)
            nc.vector.memset(rows[:, :, :, S - 1:S], 1.0)
            nc.vector.memset(eps[:, :], EPS)
            nc.vector.memset(zeros[:, :], 0.0)
            nc.vector.memset(blank[:, :], 0.0)
            ordered(nc.vector.memset(sums[:, :], 0.0))
            dve.wait_ge(consts_ready, CONSTS)
            nc.vector.tensor_copy(iota, iota_sb[:, :])
            dve.wait_ge(dst_loaded, 3 * DMA)
            ordered(nc.vector.tensor_copy(dst_rel[:, :, :], dst_all))
            nc.vector.tensor_reduce(ends[:, 0, :], dst_rel[:, :, :], axis=X, op=ALU.min)
            nc.vector.tensor_reduce(ends[:, 1, :], dst_rel[:, :, :], axis=X, op=ALU.max).then_inc(ends_ready, 1)

            dve.wait_ge(chunks_loaded, 2 * DMA)
            ordered(nc.vector.tensor_reduce(least[:, :], chunk_dst, axis=X, op=ALU.min))
            ordered(nc.vector.tensor_tensor(chunk_off, chunk_dst,
                                            least[:, :].rearrange("g (c a) -> g c a", a=1).to_broadcast([COUNTED, J, P]),
                                            ALU.subtract))
            ordered(nc.vector.tensor_reduce(reach[:, :], chunk_off.rearrange("g c e -> g (c e)"), axis=X, op=ALU.max))
            nc.vector.tensor_scalar(narrow[:, :], reach[:, :], float(W), None, ALU.is_lt)
            nc.vector.tensor_scalar(wide[:, :], reach[:, :], float(W), None, ALU.is_ge)
            nc.vector.tensor_scalar(chunk_tile, chunk_src, SHIFT, None, ALU.arith_shift_right)
            ordered(nc.vector.tensor_scalar(chunk_low, chunk_src, P - 1, None, ALU.bitwise_and))
            ordered(nc.vector.tensor_scalar(chunk_low_f, chunk_low, 1.0, None, ALU.add))
            ordered(nc.vector.scalar_tensor_tensor(out=chunk_off, in0=chunk_tile, scalar=float(W), in1=chunk_off,
                                                   op0=ALU.mult, op1=ALU.add))
            ordered(nc.vector.tensor_scalar(chunk_key, chunk_off, 1.0, narrow[:, 0:1], ALU.add, ALU.mult))
            nc.vector.tensor_tensor(slot_rows[:, :, :], slot_iota[:, :, :],
                                    least[:, :].rearrange("g (c a) -> g c a", a=1).to_broadcast([COUNTED, J, W]),
                                    ALU.add).then_inc(keys_made, 1)

            dve.wait_ge(ends_turned, 1)
            for e, op in ((0, ALU.min), (1, ALU.max)):
                nc.vector.tensor_reduce(group_ends[:, e, 0:1], ends_ps[:, e * 2 * P:e * 2 * P + P], axis=X, op=op)
                last = nc.vector.tensor_reduce(group_ends[0:GROUPS - P, e, 1:2],
                                               ends_ps[0:GROUPS - P, e * 2 * P + P:(e + 1) * 2 * P], axis=X, op=op)
            ordered(last)
            nc.vector.tensor_copy(masks[:, 0, 0, :], group_ends[:, 0, 0:1].to_broadcast([P, P]))
            nc.vector.tensor_copy(masks[0:GROUPS - P, 1, 0, :], group_ends[0:GROUPS - P, 0, 1:2]
                                  .to_broadcast([GROUPS - P, P])).then_inc(group_ends_ready, 1)
            dve.wait_ge(group_ends_turned, 1)
            ordered(nc.vector.tensor_copy(span[:, :, :],
                                          lists_ps[0:1, 0:2 * GROUPS].rearrange("p (e g) -> p g e", e=2)))
            ordered(nc.vector.tensor_tensor(span[:, :, 1], span[:, :, 1], span[:, :, 0], ALU.subtract))
            ordered(nc.vector.tensor_scalar(span[:, :, 1], span[:, :, 1], SHIFT, None, ALU.arith_shift_right))
            nc.vector.tensor_scalar(span[:, :, 1], span[:, :, 1], 1, None, ALU.add)
            nc.vector.tensor_tensor(dst_rel[:, :, :], dst_rel[:, :, :],
                                    base_ps.rearrange("p (g a) -> p g a", a=1).to_broadcast([P, GROUPS, J]),
                                    ALU.subtract)
            nc.vector.tensor_copy(wide_row[:, :], lists_ps[0:1, BANK:BANK + COUNTED])
            ordered(nc.vector.tensor_reduce(any_wide_f[:, :], lists_ps[0:1, BANK:BANK + COUNTED], axis=X, op=ALU.max))
            nc.vector.tensor_copy(any_wide[:, :], any_wide_f[:, :]).then_inc(group_ends_ready, 1)
            dve.wait_ge(keys_turned, 1)
            ordered(nc.vector.tensor_copy(slot_node[:, :], turn_ps[0:SLOTS, 0:COUNTED]))
            nc.vector.tensor_tensor(slot_node[:, :], slot_node[:, :], base_ps[0:SLOTS, 0:COUNTED], ALU.subtract)
            for q in range(-(-2 * J // KEYS_IN_BANK)):
                some_keys = keys[:, :, :, :].rearrange("p k c g -> p (k c g)")[
                    :, q * KEYS_IN_BANK * COUNTED:min(2 * J, (q + 1) * KEYS_IN_BANK) * COUNTED]
                last = nc.vector.tensor_copy(some_keys, build[:, q, 0:some_keys.shape[1]])
            last.then_inc(lists_ready, 1)
            dve.wait_ge(lists_ready, 1)

            pairs = dve.alloc_register("dve_pairs")
            before = dve.alloc_register("dve_before")
            slot_pairs = dve.alloc_register("dve_slot_pairs")
            dve.reg_mov(pairs, 0)
            dve.reg_mov(slot_pairs, 0)
            span_regs = [dve.alloc_register(f"dve_span{n}") for n in range(2 * RING)]
            slot_span_regs = [dve.alloc_register(f"dve_slot_span{n}") for n in range(2 * PER_ROUND)]

            def take_part(layer, k, node):
                width = D if layer else S
                dve.wait_ge(part_ready, k + 1)
                dve.wait_ge(part_taken, k + 1)
                here = sums[0:width, bass.ds(node, P)]
                return nc.vector.tensor_tensor(here, part[0:width, (k + 1) % 2, 0:P], here, ALU.add)

            def load_spans(regs, g, count):
                dve.load(regs[0:2 * count], span[0:1, bass.ds(g, count), :])

            def mask_pairs(layer, span_of_group, make_mask, between=None):
                node_reg, windows_reg = span_of_group
                windows = dve.snap(windows_reg, min_val=1, max_val=TILES)

                def mask_pair(w):
                    k = dve.snap(pairs, min_val=0, max_val=MAX_PAIRS)
                    make_mask(k, w).then_inc(masks_ready, 1)
                    take_part(layer, k, dve.snap(before, min_val=0, max_val=NP - 1)).then_inc(part_taken, 1)
                    dve.reg_add(before, node_reg, 0)
                    dve.reg_add(node_reg, node_reg, P)
                    dve.reg_add(pairs, pairs, 1)

                mask_pair(0)
                if between:
                    between()
                with dve.If(windows > 1):
                    with dve.Fori(1, windows) as w:
                        mask_pair(w)

            def mask_group(layer, g, span, between=None):
                def make_mask(k, w):
                    return nc.vector.scalar_tensor_tensor(
                        out=masks[:, k % 2, :, :],
                        in0=dst_rel[:, g, :].rearrange("p (j a) -> p j a", a=1).to_broadcast([P, J, P]),
                        scalar=window_base[:, bass.ds(w, 1)],
                        in1=iota.rearrange("p (a n) -> p a n", a=1).to_broadcast([P, J, P]),
                        op0=ALU.subtract, op1=ALU.is_equal)
                mask_pairs(layer, span, make_mask, between)

            def mask_slots(layer, i, s, span):
                g = i * PER_ROUND + s
                dve.wait_ge(slots_summed, i * PER_ROUND + ((layer - 1) * COUNTED + s + 1))
                dve.wait_ge(part_ready, dve.snap(slot_pairs, min_val=0, max_val=MAX_PAIRS) + 1)
                nc.vector.tensor_reduce(slot_sums[:, :], slots_ps.rearrange("p (k d) -> p d k", k=PARTS),
                                        axis=X, op=ALU.add).then_inc(slots_taken, 1)

                def make_mask(k, w):
                    return nc.vector.scalar_tensor_tensor(
                        out=masks[0:SLOTS, k % 2, 0, :],
                        in0=slot_node[:, bass.ds(g, 1)].to_broadcast([SLOTS, P]),
                        scalar=window_base[0:SLOTS, bass.ds(w, 1)],
                        in1=iota[0:SLOTS, :], op0=ALU.subtract, op1=ALU.is_equal)
                mask_pairs(layer, span, make_mask)
                dve.reg_add(slot_pairs, pairs, 0)

            def make_onehots(i, s):
                g = i * BPER_ROUND + s // 2
                first, width = (0, 2 * KEYS) if s % 2 == 0 else (2 * KEYS, KEYS)
                for c in range(J):
                    n = s * J + c
                    turn = n % 2
                    if not isinstance(i, int) or i or n >= 2:
                        dve.wait_ge(chunk_built, i * (RING * J) + (n - 1))
                    nc.vector.tensor_scalar(is_low[:, turn, :], from_one[:, 0:P], keys[:, 1, c, bass.ds(g, 1)],
                                            None, ALU.is_equal)
                    nc.vector.tensor_scalar(is_key[:, turn, 0:width], from_one[:, first:first + width],
                                            keys[:, 0, c, bass.ds(g, 1)], None,
                                            ALU.is_equal).then_inc(onehots_ready, 1)

            def node_batch(layer, i, slot):
                done = layer * BATCHES
                n = 2 * i + slot

                def ordered_step(ins, step):
                    ins.then_inc(node_step, 1)
                    dve.wait_ge(node_step, n * STEPS + (done * STEPS + step))

                dve.wait_ge(conv_ready, n + (done + 3))
                ordered_step(nc.vector.tensor_copy(deg[:, :], rest_ps[slot][:, :, D]), 1)
                ordered_step(nc.vector.tensor_tensor(left[:, :, :], own_ps[slot], per_node(deg), ALU.mult), 2)
                if layer < LAYERS - 1:
                    dve.wait_ge(nodes_ready, n + (done + 1))
                ins = nc.vector.tensor_tensor(z[:, :, :], left[:, :, :], rest_ps[slot][:, :, 0:D], ALU.add)
                ins.then_inc(conv_taken, 1)
                dve.wait_ge(conv_taken, n + (done + 3))
                if layer < LAYERS - 1:
                    to = [parts[:, bass.ds(n * BT, BT), k, :] for k in range(PARTS)]
                    ordered_step(nc.vector.tensor_scalar(to[0], z[:, :, :], 0.0, None, ALU.max), 3)
                    ordered_step(nc.vector.scalar_tensor_tensor(
                        out=left[:, :, :], in0=z[:, :, :], scalar=0.0, in1=to[0], op0=ALU.max, op1=ALU.subtract), 4)
                    ordered_step(nc.vector.tensor_copy(to[1], left[:, :, :]), 5)
                    ordered_step(nc.vector.tensor_tensor(to[2], left[:, :, :], to[1], ALU.subtract), 6)
                else:
                    dve.wait_ge(x_loaded[slot], (i + 1) * 2 * DMA)
                    ordered_step(nc.vector.tensor_tensor(z[:, :, :], z[:, :, :], x_rows[:, slot, :, :], ALU.add), 3)
                    ordered_step(nc.vector.tensor_reduce(mean[:, :], z[:, :, :], axis=X, op=ALU.add), 4)
                    ordered_step(nc.vector.scalar_tensor_tensor(
                        out=z[:, :, :], in0=per_node(mean), scalar=-1.0 / D, in1=z[:, :, :],
                        op0=ALU.mult, op1=ALU.add), 5)
                    nc.vector.tensor_tensor(left[:, :, :], z[:, :, :], z[:, :, :], ALU.mult).then_inc(square_ready, 1)
                    dve.wait_ge(square_ready, n + 1)
                    nc.vector.tensor_reduce(var[:, :], left[:, :, :], axis=X, op=ALU.add).then_inc(var_ready, 1)
                    dve.wait_ge(std_ready, n + 1)
                    ordered_step(nc.vector.reciprocal(rstd[:, :], std[:, :]), 6)
                    dve.wait_ge(nodes_stored[slot], (i * 2 + layer * BATCHES // 2) * DMA)
                    nc.vector.tensor_tensor(node_rows[:, slot, :, :], z[:, :, :], per_node(rstd),
                                            ALU.mult).then_inc(nodes_ready, 1)

            for layer in range(LAYERS):
                ordered(nc.vector.memset(part[:, :, 0:P], 0.0))
                dve.reg_mov(before, 0)
                if layer:
                    dve.wait_ge(sums_cleared, layer * BATCHES)

                def groups_of_round(i, counted):
                    first_group = COUNTED if layer else 0
                    load_spans(span_regs, i * RING + first_group, RING)
                    if layer and counted:
                        load_spans(slot_span_regs, i * PER_ROUND, counted)
                    for s in range(RING):
                        between = (lambda: make_onehots(i, s)) if layer == 0 and s < counted else None
                        mask_group(layer, i * RING + (s + first_group), span_regs[2 * s:2 * s + 2], between)
                        if layer and s < counted:
                            mask_slots(layer, i, s, slot_span_regs[2 * s:2 * s + 2])

                if layer == 0:
                    groups_of_round(0, RING)
                    with dve.Fori(1, PEELED) as i:
                        groups_of_round(i, RING)
                    for i in range(PEELED, ROUNDS0):
                        groups_of_round(i, slots_building(i))
                else:
                    with dve.Fori(0, CROUNDS) as i:
                        groups_of_round(i, PER_ROUND)
                    groups_of_round(CROUNDS, CREST)
                    for i in range(CROUNDS + 1, ROUNDS):
                        groups_of_round(i, 0)
                if layer:
                    some = dve.value_load(any_wide[0:1, 0:1], min_val=0, max_val=1)
                    with dve.If(some > 0):
                        with dve.Fori(0, COUNTED) as g:
                            is_wide = dve.value_load(wide_row[0:1, bass.ds(g, 1)], min_val=0, max_val=1)
                            with dve.If(is_wide > 0):
                                load_spans(span_regs, g, 1)
                                mask_group(layer, g, span_regs[0:2])
                take_part(layer, dve.snap(pairs, min_val=0, max_val=MAX_PAIRS),
                          dve.snap(before, min_val=0, max_val=NP - 1)).then_inc(layer_summed, 1)
                with dve.Fori(0, BATCHES // 2) as i:
                    for slot in range(2):
                        node_batch(layer, i, slot)

        @block.tensor
        def _(pe):
            for handed, count in handed_back["PE"]:
                pe.sem_inc(handed, count)
            pe.wait_ge(consts_ready, CONSTS)
            pe.wait_ge(ends_ready, 1)
            for e in range(2):
                nc.tensor.transpose(ends_ps[0:P, e * 2 * P:e * 2 * P + P], ends[:, e, 0:P], ident[:, :])
                last = nc.tensor.transpose(ends_ps[0:GROUPS - P, e * 2 * P + P:(e + 1) * 2 * P],
                                           ends[:, e, P:GROUPS], ident[:, :])
            last.then_inc(ends_turned, 1)
            pe.wait_ge(group_ends_ready, 1)
            pe.wait_ge(keys_made, 1)
            nc.tensor.matmul(base_ps[:, 0:P], masks[:, 0, 0, :], ident[:, :], start=True, stop=True)
            nc.tensor.matmul(base_ps[:, P:GROUPS], masks[0:GROUPS - P, 1, 0, :],
                             ident[0:GROUPS - P, 0:GROUPS - P], start=True, stop=True)
            for e in range(2):
                nc.tensor.transpose(lists_ps[0:1, e * GROUPS:e * GROUPS + P], group_ends[:, e, 0:1], ident[:, :])
                nc.tensor.transpose(lists_ps[0:1, e * GROUPS + P:(e + 1) * GROUPS],
                                    group_ends[0:GROUPS - P, e, 1:2], ident[0:GROUPS - P, 0:GROUPS - P])
            nc.tensor.transpose(lists_ps[0:1, BANK:BANK + COUNTED], wide[:, :],
                                ident[0:COUNTED, 0:COUNTED]).then_inc(group_ends_turned, 1)
            pe.wait_ge(group_ends_ready, 2)
            for k, what in enumerate((chunk_key, chunk_low_f)):
                for c in range(J):
                    q, at = divmod(k * J + c, KEYS_IN_BANK)
                    nc.tensor.transpose(build[:, q, at * COUNTED:(at + 1) * COUNTED], what[:, c, :], ident[0:COUNTED, 0:COUNTED])
            nc.tensor.transpose(turn_ps[0:SLOTS, 0:COUNTED], slot_rows[:, :, :].rearrange("g c w -> g (c w)"),
                                ident[0:COUNTED, 0:COUNTED]).then_inc(keys_turned, 1)

            pe.wait_ge(lists_ready, 1)
            pe.wait_ge(w_loaded, 3 * LAYERS * DMA)
            pairs = pe.alloc_register("pe_pairs")
            wides = pe.alloc_register("pe_wides")
            pe.reg_mov(pairs, 0)
            pe.reg_mov(wides, 0)
            span_regs = [pe.alloc_register(f"pe_span{n}") for n in range(2 * RING)]
            slot_span_regs = [pe.alloc_register(f"pe_slot_span{n}") for n in range(2 * PER_ROUND)]

            def load_spans(regs, g, count):
                pe.load(regs[0:2 * count], span[0:1, bass.ds(g, count), :])

            def mark(layer):
                spare = build[0:1, 3, BANK - 1:BANK] if layer else turn_ps[0:1, BANK - 1:BANK]
                return nc.tensor.matmul(spare, blank[:, :], blank[:, :], start=True, stop=True)

            def sum_pair(width, operands, between=None):
                k = pe.snap(pairs, min_val=0, max_val=MAX_PAIRS)
                pe.wait_ge(masks_ready, k + 1)
                pe.wait_ge(part_taken, k + 1)
                products = operands(k % 2)
                for j, (values, rhs) in enumerate(products):
                    mm = nc.tensor.matmul(part[0:width, k % 2, 0:P], values, rhs,
                                          start=(j == 0), stop=(j == len(products) - 1))
                    if j == len(products) - 1:
                        mm.then_inc(part_ready, 1)
                    if between:
                        between(j)
                pe.reg_add(pairs, pairs, 1)

            def sum_pairs(windows_reg, width, operands, between=None):
                windows = pe.snap(windows_reg, min_val=1, max_val=TILES)
                sum_pair(width, operands, between)
                with pe.If(windows > 1):
                    with pe.Fori(1, windows):
                        sum_pair(width, operands)

            def sum_rows(layer, windows_reg, s, between=None):
                width = D if layer else S
                sum_pairs(windows_reg, width, lambda turn: [(rows[:, s, j, 0:width], masks[:, turn, j, :]) for j in range(J)],
                          between)

            def sum_slots(windows_reg):
                sum_pairs(windows_reg, D, lambda turn: [(slot_sums[:, :], masks[0:SLOTS, turn, 0, :])])

            def build_counts(i, s):
                def build_chunk(c):
                    n = s * J + c
                    turn = n % 2
                    pe.wait_ge(onehots_ready, i * (RING * J) + (n + 1))
                    if not isinstance(i, int) or i or n >= 2:
                        pe.wait_ge(chunk_kept, i * (RING * J) + (n - 1))
                    for q in range(2 - s % 2):
                        last = nc.tensor.matmul(build[:, 2 * turn + q, 0:KEYS], is_low[:, turn, :],
                                                is_key[:, turn, q * KEYS:(q + 1) * KEYS],
                                                start=True, stop=True)
                    last.then_inc(chunk_built, 1)
                return build_chunk

            def apply_counts(layer, i, s):
                pe.wait_ge(slots_taken, i * PER_ROUND + ((layer - 1) * COUNTED + s + 1))
                for third, tiles in enumerate(THIRDS):
                    u = len(THIRDS) * s + third
                    r = u % CRING
                    pe.wait_ge(block_loaded[r], (placed_before(layer, i, u) + 1) * DMA)
                    for t in tiles:
                        last = nc.tensor.matmul(slots_ps, blocks[:, r, t - tiles[0], :],
                                                parts[:, t, :, :].rearrange("p k d -> p (k d)"),
                                                start=(t == 0), stop=(t == TILES - 1))
                    if t < TILES - 1:
                        last.then_inc(block_used[r], 1)
                last.then_inc(slots_summed, 1)
                mark(layer).then_inc(block_used[r], 1)

            def groups_of_round(layer, i, counted):
                load_spans(span_regs, i * RING + (COUNTED if layer else 0), RING)
                if layer and counted:
                    load_spans(slot_span_regs, i * PER_ROUND, counted)
                uses = pe.compute_val(i + (USES[layer] + 1))
                landed = pe.compute_val(uses * (J * DMA))
                for s in range(RING):
                    if layer and s < counted:
                        apply_counts(layer, i, s)
                    pe.wait_ge(lists_ready, 1)
                    pe.wait_ge(rows_landed[s], landed)
                    if layer == 0:
                        pe.wait_ge(attr_copied[s], uses)
                    between = build_counts(i, s) if layer == 0 and s < counted else None
                    sum_rows(layer, span_regs[2 * s + 1], s, between)
                    mark(layer).then_inc(rows_used[s], 1)
                    if layer and s < counted:
                        sum_slots(slot_span_regs[2 * s + 1])

            for layer in range(LAYERS):
                if layer == 0:
                    groups_of_round(0, 0, RING)
                    with pe.Fori(1, PEELED) as i:
                        groups_of_round(0, i, RING)
                    for i in range(PEELED, ROUNDS0):
                        groups_of_round(0, i, slots_building(i))
                else:
                    pe.wait_ge(node_step, layer * BATCHES * STEPS)
                    with pe.Fori(0, CROUNDS) as i:
                        groups_of_round(layer, i, PER_ROUND)
                    groups_of_round(layer, CROUNDS, CREST)
                    for i in range(CROUNDS + 1, ROUNDS):
                        groups_of_round(layer, i, 0)
                if layer:
                    some = pe.value_load(any_wide[0:1, 0:1], min_val=0, max_val=1)
                    with pe.If(some > 0):
                        with pe.Fori(0, COUNTED) as g:
                            is_wide = pe.value_load(wide_row[0:1, bass.ds(g, 1)], min_val=0, max_val=1)
                            with pe.If(is_wide > 0):
                                landed = pe.compute_val((pe.snap(wides, min_val=0, max_val=LAYERS * COUNTED) + 1) * (J * DMA))
                                pe.wait_ge(lists_ready, 1)
                                pe.wait_ge(wide_landed, landed)
                                load_spans(span_regs, g, 1)
                                sum_rows(layer, span_regs[1], 0)
                                mark(layer).then_inc(wide_used, 1)
                                pe.reg_add(wides, wides, 1)

                def turn_h(b, loaded, slot):
                    kept = pe.compute_val(b + layer * BATCHES) if not isinstance(b, int) or b + layer else None
                    pe.wait_ge(consts_ready, CONSTS)
                    pe.wait_ge(h_loaded[slot], loaded)
                    if kept is not None:
                        pe.wait_ge(h_kept, kept)
                    for t in range(BT):
                        last = nc.tensor.transpose(turn_h_ps[0:D, t * P:(t + 1) * P], h_rows[:, slot, t, :],
                                                   ident[:, :])
                    last.then_inc(h_in_psum, 1)

                def node_batch(i, slot):
                    b = pe.compute_val(2 * i + slot)
                    kept = pe.compute_val(b + (layer * BATCHES + 1))
                    if not isinstance(i, int) or 2 * i + slot + 1 < BATCHES:
                        ahead = pe.compute_val((i + slot + (layer * BATCHES // 2 + 1)) * (2 * DMA))
                        turn_h(pe.compute_val(b + 1), ahead, 1 - slot)
                    pe.wait_ge(w_loaded, 3 * LAYERS * DMA)
                    pe.wait_ge(h_kept, kept)
                    pe.wait_ge(sums_kept, kept)
                    pe.wait_ge(conv_taken, kept)
                    for t in range(BT):
                        nc.tensor.matmul(own_ps[slot][:, t, :], h_turned[:, slot, t * P:(t + 1) * P],
                                         w_own[layer][:, :], start=True, stop=True)
                        last = nc.tensor.matmul(rest_ps[slot][:, t, :], batch_sums[:, slot, t * P:(t + 1) * P],
                                                w_sum[layer][:, :], start=True, stop=True)
                    last.then_inc(conv_ready, 1)

                pe.wait_ge(layer_summed, layer + 1)
                turn_h(0, (layer * BATCHES // 2 + 1) * (2 * DMA), 0)
                with pe.Fori(0, BATCHES // 2 - 1) as i:
                    for slot in range(2):
                        node_batch(i, slot)
                for slot in range(2):
                    node_batch(BATCHES // 2 - 1, slot)


_INS = ["x", "src", "dst", "edge_attr_16", "L0_gnn_W1", "L0_gnn_b1", "L0_gnn_W2", "L0_gnn_b2",
        "L0_gnn_W3", "L0_gnn_b3"]


def kernel(**inputs):
    import numpy as _np
    import concourse.bacc as _bacc
    from concourse import mybir as _mybir
    from concourse.bass_utils import run_bass_kernel_spmd as _run

    nc = _bacc.Bacc("TRN2", target_bir_lowering=False, num_devices=1)
    arrays, aps = {}, {}
    for name in _INS:
        a = _np.ascontiguousarray(inputs[name])
        arrays[f"in_{name}"] = a
        aps[name] = nc.dram_tensor(f"in_{name}", a.shape, _mybir.dt.from_np(a.dtype), kind="ExternalInput").ap()
    out = nc.dram_tensor("out_0", inputs["x"].shape, _mybir.dt.float32, kind="ExternalOutput").ap()
    weights = [(aps[f"L0_gnn_W{n}"], aps[f"L0_gnn_b{n}"]) for n in (1, 2, 3)]
    gnn_kernel(nc, aps["x"], aps["src"], aps["dst"], aps["edge_attr_16"], weights, out)
    r = _run(nc, [arrays], core_ids=[0])
    return r.results[0]["out_0"]
```
